# Optimizing a Trainium2 kernel written in Bass

```python
import numpy as np
import jax
import jax.numpy as jnp

def _softmax(x, axis=-1):
    return jax.nn.softmax(x, axis=axis)

def _gelu(x):
    return jax.nn.gelu(x, approximate=True)

def _silu(x):
    return jax.nn.silu(x)

def _sigmoid(x):
    return jax.nn.sigmoid(x)

def _layernorm(x, axis=-1, eps=1e-05):
    m = jnp.mean(x, axis=axis, keepdims=True)
    v = jnp.var(x, axis=axis, keepdims=True)
    return (x - m) / jnp.sqrt(v + eps)

def _scatter_add(tgt, idx, src, axis=0):
    return tgt.at[idx].add(src)

def _segment_sum(src, seg, n):
    return jax.ops.segment_sum(src, seg, n)
kernel_name = 'mk_seq_preln_d1_jaxref_r8_2cdfed'

def setup_inputs(seed: int=0):
    np.random.seed(seed)
    _w = jnp.asarray

    def _L0_attn_setup():
        import jax, jax.numpy as jnp
        import numpy as np
        N_EMBD = 128
        N_HEAD = 16
        HEAD_SIZE = 64
        LN_EPS = 0.001
        key = jax.random.key(seed)
        ks = jax.random.split(key, 7)
        B, S, D, H, E = (4, 256, N_EMBD, N_HEAD, HEAD_SIZE)
        x = jax.random.normal(ks[0], (B, S, D), dtype=jnp.float32)
        scale = 1.0 / np.sqrt(D)
        Wq = jax.random.normal(ks[1], (H, D, E), dtype=jnp.float32) * scale
        Wk = jax.random.normal(ks[2], (H, D, E), dtype=jnp.float32) * scale
        Wv = jax.random.normal(ks[3], (H, D, E), dtype=jnp.float32) * scale
        Wo = jax.random.normal(ks[4], (H * E, D), dtype=jnp.float32) * scale
        gamma = jnp.ones((D,), dtype=jnp.float32)
        beta = jnp.zeros((D,), dtype=jnp.float32)
        return {'x': x, 'Wq': Wq, 'Wk': Wk, 'Wv': Wv, 'Wo': Wo, 'gamma': gamma, 'beta': beta}
    _L0_attn_in = _L0_attn_setup()

    def _L0_ffn_setup():
        import jax, jax.numpy as jnp
        import numpy as np
        TOP_K = 8
        NUM_EXPERTS = 32
        HIDDEN = 128
        EXPERT_DIM = 64
        key = jax.random.key(seed)
        k1, k2, k3, k4 = jax.random.split(key, 4)
        hidden_states = jax.random.normal(k1, (1, 256, HIDDEN), dtype=jnp.float32)
        gate_w = jax.random.normal(k2, (NUM_EXPERTS, HIDDEN), dtype=jnp.float32) * 0.02
        gate_up_w = jax.random.normal(k3, (NUM_EXPERTS, 2 * EXPERT_DIM, HIDDEN), dtype=jnp.float32) * 0.02
        down_w = jax.random.normal(k4, (NUM_EXPERTS, HIDDEN, EXPERT_DIM), dtype=jnp.float32) * 0.02
        return {'hidden_states': hidden_states, 'gate_w': gate_w, 'gate_up_w': gate_up_w, 'down_w': down_w}
    _L0_ffn_in = _L0_ffn_setup()
    _d = {'L0_attn_x': _L0_attn_in['x'], 'L0_attn_Wq': _L0_attn_in['Wq'], 'L0_attn_Wk': _L0_attn_in['Wk'], 'L0_attn_Wv': _L0_attn_in['Wv'], 'L0_attn_Wo': _L0_attn_in['Wo'], 'L0_attn_gamma': _L0_attn_in['gamma'], 'L0_attn_beta': _L0_attn_in['beta'], 'L0_ffn_gate_w': _L0_ffn_in['gate_w'], 'L0_ffn_gate_up_w': _L0_ffn_in['gate_up_w'], 'L0_ffn_down_w': _L0_ffn_in['down_w']}
    _x0 = _d['L0_attn_x']
    _d['L0_attn_x'] = jax.random.normal(jax.random.fold_in(jax.random.key(seed), 1), (16, 512, 128), dtype=_x0.dtype)
    del _x0
    return _d

def reference(L0_attn_x, L0_attn_Wq, L0_attn_Wk, L0_attn_Wv, L0_attn_Wo, L0_attn_gamma, L0_attn_beta, L0_ffn_gate_w, L0_ffn_gate_up_w, L0_ffn_down_w):

    def _L0_attn_ref(x, Wq, Wk, Wv, Wo, gamma, beta):
        import jax, jax.numpy as jnp
        import numpy as np
        N_EMBD = 128
        N_HEAD = 16
        HEAD_SIZE = 64
        LN_EPS = 0.001
        B, S, D = x.shape
        H, _, E = Wq.shape
        q = jnp.einsum('bsd,hde->bhse', x, Wq)
        k = jnp.einsum('bsd,hde->bhse', x, Wk)
        v = jnp.einsum('bsd,hde->bhse', x, Wv)
        scores = jnp.einsum('bhse,bhte->bhst', q, k)
        causal = jnp.tril(jnp.ones((S, S), dtype=bool))
        scores = jnp.where(causal, scores / jnp.sqrt(jnp.float32(E)), jnp.float32(-jnp.inf))
        attn = jax.nn.softmax(scores, axis=-1)
        out = jnp.einsum('bhst,bhte->bhse', attn, v)
        heads = out.transpose(0, 2, 1, 3).reshape(B, S, H * E)
        y = x + heads @ Wo
        mu = jnp.mean(y, axis=-1, keepdims=True)
        var = jnp.mean(jnp.square(y - mu), axis=-1, keepdims=True)
        y = (y - mu) * jax.lax.rsqrt(var + LN_EPS) * gamma + beta
        return y

    def _L0_ffn_ref(hidden_states, gate_w, gate_up_w, down_w):
        import jax, jax.numpy as jnp
        import numpy as np
        TOP_K = 8
        NUM_EXPERTS = 32
        HIDDEN = 128
        EXPERT_DIM = 64
        B, S, H = hidden_states.shape
        x = hidden_states.reshape(-1, H)
        logits = x @ gate_w.T
        probs = jax.nn.softmax(logits.astype(jnp.float32), axis=-1)
        top_w, top_idx = jax.lax.top_k(probs, TOP_K)
        top_w = top_w / jnp.sum(top_w, axis=-1, keepdims=True)
        top_w = top_w.astype(x.dtype)
        comb = jnp.sum(jax.nn.one_hot(top_idx, NUM_EXPERTS, dtype=x.dtype) * top_w[..., None], axis=1)

        def body(acc, ws):
            guw, dw, w_e = ws
            gu = x @ guw.T
            g, u = jnp.split(gu, 2, axis=-1)
            y = u * jax.nn.silu(g) @ dw.T
            return (acc + y * w_e[:, None], None)
        init = jnp.zeros_like(x)
        out, _ = jax.lax.scan(body, init, (gate_up_w, down_w, comb.T))
        return out.reshape(B, S, H)
    x = L0_attn_x
    x = x + _L0_attn_ref(_layernorm(x, axis=-1), L0_attn_Wq, L0_attn_Wk, L0_attn_Wv, L0_attn_Wo, L0_attn_gamma, L0_attn_beta)
    x = x + _L0_ffn_ref(_layernorm(x, axis=-1), L0_ffn_gate_w, L0_ffn_gate_up_w, L0_ffn_down_w)
    return x

_drawn_inputs = setup_inputs


def setup_inputs(seed=0):
    import zlib

    import numpy as np

    out = dict(_drawn_inputs(seed))
    spreads = {'L0_attn_gamma': (1.0, 0.2), 'L0_attn_beta': (0.0, 0.1)}
    factors = {'L0_ffn_gate_w': 8.0, 'L0_ffn_gate_up_w': 8.0, 'L0_ffn_down_w': 8.0}
    for name, (base, spread) in spreads.items():
        noise = np.random.default_rng([zlib.crc32(name.encode()), seed]).standard_normal(out[name].shape)
        drawn = base * np.exp(spread * noise) if base else spread * noise
        out[name] = jnp.asarray(drawn.astype(out[name].dtype))
    for name, factor in factors.items():
        out[name] = (out[name] * factor).astype(out[name].dtype)
    return out
```

```python
from contextlib import ExitStack

import numpy as np
import concourse.bass as bass
from concourse import mybir

F32, F16, I32 = mybir.dt.float32, mybir.dt.float16, mybir.dt.int32
ALU = mybir.AluOpType
ACT = mybir.ActivationFunctionType
AX = mybir.AxisListType

P = 128
B, S, D = 16, 512, 128
H, E = 16, 64
PAIRS = H // 2
C = S // P
NE, TOPK, ED = 32, 8, 64
EP = NE // 2
GROUPS = 4
LN_EPS, ATTN_LN_EPS = 1e-5, 1e-3
MAX_UNIT = 2.0 ** 13
COMB_SHIFT = 2.0 ** -8
NEG = -3.0e38
LAG = 2
UNITS = 3
PCOLS = 1280
NPROJ = 8 + 2 * PAIRS


def prob_col(t, c):
    return {0: c * P, 1: 512 + (c - 1) * P, 2: 1024 + (c - 2) * P, 3: 896}[t]


def layer(nc, x, wq, wk, wv, wo, gamma, beta, gate, gate_up, down, ident_c, mask_c, select_c, out):
    with ExitStack() as ctx:
        def sb(name, shape, dt):
            return ctx.enter_context(nc.sbuf_tensor(name, shape, dt))

        def sem(name):
            return ctx.enter_context(nc.semaphore(name))

        ident = sb("ident", [P, P], F16)
        mask = sb("mask", [P, S], F32)
        select = sb("select", [P, EP, P], F16)
        score_ops = sb("score_ops", [P, 4, 2, PAIRS, S], F16)
        KA, KB, QA, QB = (score_ops[:, n] for n in range(4))
        raw = score_ops[:, :, :, :, :].rearrange("p a b c d -> p (a b c d)").bitcast(F32)
        WCOLS = [D * 8, D * 8, D * 8, D * 8, EP * 2 * P, EP * D, NE]
        WQ, WK, WV, WO, WGU, WD, WG = range(7)
        WAT = [sum(WCOLS[:n]) for n in range(7)]
        w_hi = sb("w_hi", [P, sum(WCOLS)], F16)
        w_lo = sb("w_lo", [P, sum(WCOLS)], F16)
        w_absmax = sb("w_absmax", [P, 8], F32)
        w_allmax = sb("w_allmax", [P, 8], F32)
        w_pow = sb("w_pow", [P, 8], F32)
        w_scale = sb("w_scale", [P, 8], F32)
        w_back = sb("w_back", [P, 8], F32)
        back = sb("back", [P, 8], F32)
        SC_SCORE, SC_Y, SC_TANH, SC_OUT, SC_GU2 = range(5)
        gam = sb("gam", [P, 1, D], F32)
        bet = sb("bet", [P, 1, D], F32)
        minus_half = sb("minus_half", [P, C], F32)

        xt = sb("xt", [P, C, D], F32)
        h32 = sb("h32", [P, C, D], F32)
        h_cur = sb("h_cur", [P, C, D], F32)
        xb_cur = sb("xb_cur", [P, C, D], F32)
        split_hl = sb("split_hl", [P, 2, C, D], F16)
        hT = sb("hT", [P, 2, S], F16)
        stats = sb("stats", [P, 3, C, 6], F32)
        mv = sb("mv", [P, 3, C, 2], F32)
        var_eps = sb("var_eps", [P, 3, C], F32)
        rstd = sb("rstd", [P, 3, C], F32)
        nat_hi = sb("nat_hi", [P, 2, 2, 2, S], F16)
        nat_lo = sb("nat_lo", [P, 2, 2, 2, S], F16)
        v_hi = sb("v_hi", [P, C, H, E + 1], F16)
        v_lo = sb("v_lo", [P, C, H, E], F16)
        max_junk = sb("max_junk", [P, 2, S], F16)
        rowmax = sb("rowmax", [P, C, H], F32)
        rowmax_hl = sb("rowmax_hl", [P, C, 2, H], F16)
        room = sb("room", [P, 6 * PCOLS], F32)

        def carve(at, slots, cols, dt):
            words = slots * cols // (1 if dt is F32 else 2)
            return room[:, at:at + words].bitcast(dt).rearrange("p (a b) -> p a b", a=slots)
        p32 = carve(0, 3, PCOLS, F32)
        p_hi, p_lo = (carve(at, 3, PCOLS, F16) for at in (3 * PCOLS, 3 * PCOLS + 3 * PCOLS // 2))
        th, up, sg, su, a32 = (carve(2 * S * n, 2, S, F32) for n in range(5))
        logits, dropped, chosen, shifted, ex, exm, comb, comb_rest = (
            carve(13 * S + n * C * NE, C, NE, F32) for n in range(8))
        a_hi, a_lo = (carve(10 * S + n * 3 * S // 2, 3, S, F16) for n in range(2))
        rden = sb("rden", [P, 2, C], F32)
        o32 = sb("o32", [P, 2, C, E], F32)
        o_hl = sb("o_hl", [P, 2, 2, C, 2 * E], F16)
        oT = sb("oT", [P, 2, 2, S], F16)
        y0 = sb("y0", [P, C, D], F32)
        x1 = sb("x1", [P, C, D], F32)
        h2T = sb("h2T", [P, 2, S], F16)
        top8 = sb("top8", [P, C, TOPK], F32)
        exsum = sb("exsum", [P, C], F32)
        exinv = sb("exinv", [P, C], F32)
        comb_parts = sb("comb_parts", [P, C, 4, NE], F16)
        combT = sb("combT", [P, S], F16)
        rowmaxT = combT[0:2 * H, :]

        S0, S1, S2, P0, P1, G0, G1, XB = (
            ctx.enter_context(nc.psum_tensor(f"bank_{n}", [P, S], F32)) for n in ("s0", "s1", "s2", "p0", "p1", "g0", "g1", "x"))
        score_banks = [S0, S1, S2]
        pv_banks = [P0, P1]
        proj_banks = [G0, G1, P0, P1]
        oT_banks = [G0, G1]
        gate_banks, up_banks, weight_banks = [S0, S1], [S2, P0], [P1, G0]

        def half(bank):
            return bank[:, :].bitcast(F16)

        waits_met = sem("waits_met")
        consts_loaded = sem("consts_loaded")
        w_loaded = sem("w_loaded")
        w_maxed = sem("w_maxed")
        w_allmaxed = sem("w_allmaxed")
        w_scaling = sem("w_scaling")
        w_scaled = sem("w_scaled")
        w_hi_done = sem("w_hi_done")
        w_lo_done = sem("w_lo_done")
        consts_set = sem("consts_set")
        pool_set = sem("pool_set")
        x_loaded, cur_copied = sem("x_loaded"), sem("cur_copied")
        diag_pair = sem("diag_pair")
        ln_stats = [sem(f"ln{n}_stats") for n in range(3)]
        ln_mv = [sem(f"ln{n}_mv") for n in range(3)]
        ln_var = [sem(f"ln{n}_var") for n in range(3)]
        ln_rstd = [sem(f"ln{n}_rstd") for n in range(3)]
        ln_out = [sem(f"ln{n}_out") for n in range(3)]
        h_hi, h_lo = sem("h_hi"), sem("h_lo")
        hT_mm, hT_ready = sem("hT_mm"), sem("hT_ready")
        proj_mm, proj_hi, proj_lo = sem("proj_mm"), sem("proj_hi"), sem("proj_lo")
        placed = [sem(f"placed{g}") for g in range(GROUPS)]
        max_mm, max_done = sem("max_mm"), sem("max_done")
        rowmax_hi, rowmax_lo = sem("rowmax_hi"), sem("rowmax_lo")
        rowmaxT_mm, rowmaxT_ready, max_placed = sem("rowmaxT_mm"), sem("rowmaxT_ready"), sem("max_placed")
        score_mm, exp_done, masked = sem("score_mm"), sem("exp_done"), sem("masked")
        p_hi_done, p_lo_dve, p_lo_pool = sem("p_hi_done"), sem("p_lo_dve"), sem("p_lo_pool")
        pv_mm, rden_done, o32_done = sem("pv_mm"), sem("rden_done"), sem("o32_done")
        o_hi_done, o_lo_done = sem("o_hi_done"), sem("o_lo_done")
        oT_mm, oT_ready, y_mm = sem("oT_mm"), sem("oT_ready"), sem("y_mm")
        y0_done, yg_done, x1_done = sem("y0_done"), sem("yg_done"), sem("x1_done")
        h2_hi, h2_lo, h2T_mm, h2T_ready = sem("h2_hi"), sem("h2_lo"), sem("h2T_mm"), sem("h2T_ready")
        logit_mm, logits_done, top_done = sem("logit_mm"), sem("logits_done"), sem("top_done")
        drop_done, chosen_done, shift_done = sem("drop_done"), sem("chosen_done"), sem("shift_done")
        ex_done, exm_done, exsum_done, exinv_done = sem("ex_done"), sem("exm_done"), sem("exsum_done"), sem("exinv_done")
        comb_done, comb_split = sem("comb_done"), sem("comb_split")
        combT_mm, combT_ready = sem("combT_mm"), sem("combT_ready")
        g_mm, u_mm, wgt_mm = sem("g_mm"), sem("u_mm"), sem("wgt_mm")
        th_done, up_done, sg_done, su_done = sem("th_done"), sem("up_done"), sem("sg_done"), sem("su_done")
        a32_done, a_hi_done, a_lo_done, down_mm = sem("a32_done"), sem("a_hi_done"), sem("a_lo_done"), sem("down_mm")
        out_ready, out_stored = sem("out_ready"), sem("out_stored")

        def wh(w, a, n):
            return w_hi[:, WAT[w] + a:WAT[w] + a + n]

        def wl(w, a, n):
            return w_lo[:, WAT[w] + a:WAT[w] + a + n]

        def wait(eng, s, value):
            if not (isinstance(value, int) and value <= 0):
                eng.wait_ge(s, value)

        def apart(eng):
            eng.sem_inc(waits_met, 1)

        block = ctx.enter_context(nc.Block())

        @block.sync
        def _(sp):
            sp.dma_start(ident[:, :], ident_c).then_inc(consts_loaded, 16)
            sp.dma_start(mask[:, :], mask_c).then_inc(consts_loaded, 16)
            sp.dma_start(select[:, :, :], select_c).then_inc(consts_loaded, 16)
            sp.dma_start(gam[:, :, :], gamma).then_inc(consts_loaded, 16)
            sp.dma_start(bet[:, :, :], beta).then_inc(consts_loaded, 16)
            for w, src in enumerate((wq, wk, wv, wo, gate_up, down, gate)):
                sp.dma_start(raw[:, WAT[w]:WAT[w] + WCOLS[w]], src).then_inc(w_loaded, 16)

            def load_x(n):
                wait(sp, ln_out[0], C * n)
                apart(sp)
                wait(sp, cur_copied, 2 * n)
                apart(sp)
                sp.dma_start(xt[:, :, :], x[bass.ds(n, 1)].rearrange("a (c p) d -> p (a c) d", p=P)).then_inc(x_loaded, 16)

            def place_qk(n):
                wait(sp, score_mm, n * UNITS * H)
                sp.wait_ge(w_lo_done, 7)
                sp.wait_ge(consts_set, 6)
                for g in range(GROUPS):
                    done = n * NPROJ + 8 + 4 * (g + 1)
                    sp.wait_ge(proj_hi, done)
                    sp.wait_ge(proj_lo, done)
                    for ab in range(2):
                        rows = slice(E * ab, E * ab + E)
                        to = slice(2 * g, 2 * g + 2)
                        k_h, q_h = nat_hi[rows, g % 2, 0], nat_hi[rows, g % 2, 1]
                        k_l, q_l = nat_lo[rows, g % 2, 0], nat_lo[rows, g % 2, 1]
                        for dst, lower, src in ((KA, 0, k_h), (KA, 1, k_l), (KB, 0, k_h), (QA, 0, q_h), (QA, 1, q_h), (QB, 0, q_l)):
                            sp.dma_start(dst[E * lower:E * lower + E, ab, to, :], src).then_inc(placed[g], 16)

            def place_max(n):
                sp.wait_ge(rowmaxT_ready, n + 1)
                for part in range(2):
                    sp.dma_start(QB[E + part:E + part + 1].rearrange("a b p s -> a (b p) s"),
                                 rowmaxT[H * part:H * part + H, :]).then_inc(max_placed, 16)

            def store(n):
                sp.wait_ge(out_ready, n + 1)
                apart(sp)
                sp.dma_start(out[bass.ds(n, 1)].rearrange("a (c p) d -> p (a c) d", p=P), y0[:, :, :]).then_inc(out_stored, 16)

            load_x(0)
            place_qk(0)
            load_x(1)
            place_max(0)
            with sp.Fori(1, B - 1) as i:
                place_qk(i)
                load_x(i + 1)
                store(i - 1)
                place_max(i)
            place_qk(B - 1)
            store(B - 2)
            place_max(B - 1)
            store(B - 1)
            sp.wait_ge(out_stored, 16 * B)

        @block.tensor
        def _(pe):
            def mm(dst, lhsT, rhs, start, stop, shared=False):
                return pe.matmul(dst, lhsT, rhs, start=start, stop=stop, skip_group_check=shared)

            def product(dst, l_hi, l_lo, r_hi, r_lo, start=True, stop=True, shared=False):
                mm(dst, l_hi, r_hi, start, False, shared)
                mm(dst, l_hi, r_lo, False, False, shared)
                return mm(dst, l_lo, r_hi, False, stop, shared)

            def transpose_split(dst, hi_lo):
                for part in range(2):
                    for c in range(C):
                        last = pe.transpose(half(dst)[:, part * S + c * P:part * S + c * P + P], hi_lo[:, part, c, :], ident[:, :])
                return last

            def project(n):
                wait(pe, oT_ready, n * PAIRS)
                pe.wait_ge(h_lo, n + 1)
                transpose_split(G0, split_hl).then_inc(hT_mm, 1)
                pe.wait_ge(hT_ready, n + 1)
                wait(pe, o32_done, n * H)
                for k in range(NPROJ):
                    bank = proj_banks[k % 4]
                    if k >= 4:
                        pe.wait_ge(proj_lo, n * NPROJ + k - 3)
                    if k < 8:
                        c, side = k // 2, k % 2
                        hc = slice(c * P, c * P + P)
                        last = product(bank[:, :], hT[:, 0, hc], hT[:, 1, hc], wh(WV, side * S, S), wl(WV, side * S, S))
                    else:
                        pair, w = (k - 8) // 2, (WK, WQ)[k % 2]
                        last = product(bank[:, :], wh(w, pair * P, P), wl(w, pair * P, P), hT[:, 0, :], hT[:, 1, :])
                    last.then_inc(proj_mm, 1)

            def row_maxima(n):
                wait(pe, sg_done, n * EP)
                wait(pe, up_done, n * EP)
                for h in range(H):
                    pair, ab = h // 2, h % 2
                    if h % 4 == 0:
                        pe.wait_ge(placed[h // 4], 192 * (n + 1))
                    for c in range(C):
                        k = h * C + c
                        if k >= UNITS:
                            pe.wait_ge(max_done, n * H * C + k - 2)
                        cols = (c + 1) * P
                        mm(score_banks[k % 3][:, 0:cols], QA[:, ab, pair, c * P:c * P + P], KA[:, ab, pair, 0:cols],
                           True, True).then_inc(max_mm, 1)
                wait(pe, a32_done, n * EP)
                pe.wait_ge(rowmax_lo, n + 1)
                for c in range(C):
                    last = pe.transpose(half(G0)[0:2 * H, c * P:c * P + P],
                                        rowmax_hl[:, c].rearrange("p a h -> p (a h)"), ident[:, :])
                last.then_inc(rowmaxT_mm, 1)

            def scores(n, h):
                pair, ab = h // 2, h % 2
                for u, chunks in enumerate(((0,), (1, 3), (2,))):
                    k = h * UNITS + u
                    if k >= UNITS:
                        pe.wait_ge(exp_done, n * H * UNITS + k - 2)
                    for t in chunks:
                        cols, at = S - t * P, (384 if t == 3 else 0)
                        dst = score_banks[u][:, at:at + cols]
                        keys = slice(t * P, t * P + P)
                        mm(dst, KA[:, ab, pair, keys], QA[:, ab, pair, t * P:S], True, False)
                        last = mm(dst, KB[:, ab, pair, keys], QB[:, ab, pair, t * P:S], False, True)
                    last.then_inc(score_mm, 1)

            def times_v(n, h):
                if h >= 2:
                    pe.wait_ge(o32_done, n * H + h - 1)
                pe.wait_ge(p_lo_dve, n * H + h + 1)
                pe.wait_ge(p_lo_pool, n * H + h + 1)
                bank = pv_banks[h % 2]
                for c in range(C):
                    dst = bank[:, c * (E + 1):(c + 1) * (E + 1)]
                    for t in range(c + 1):
                        at = prob_col(t, c)
                        ph, pl = p_hi[:, h % 3, at:at + P], p_lo[:, h % 3, at:at + P]
                        mm(dst, ph, v_hi[:, t, h, :], t == 0, False)
                        mm(dst[:, 0:E], ph, v_lo[:, t, h, :], False, False)
                        last = mm(dst, pl, v_hi[:, t, h, :], False, t == c)
                last.then_inc(pv_mm, 1)

            def turn_heads(n, q):
                if q >= 2:
                    pe.wait_ge(oT_ready, n * PAIRS + q - 1)
                pe.wait_ge(o_lo_done, n * H + 2 * q + 2)
                pe.wait_ge(o_hi_done, n * H + 2 * q + 2)
                transpose_split(oT_banks[q % 2], o_hl[:, q % 2]).then_inc(oT_mm, 1)

            def times_wo(n, q):
                pe.wait_ge(oT_ready, n * PAIRS + q + 1)
                for c in range(C):
                    tok = slice(c * P, c * P + P)
                    last = product(XB[:, c * P:c * P + P], oT[:, q % 2, 0, tok], oT[:, q % 2, 1, tok],
                                   wh(WO, q * P, P), wl(WO, q * P, P), q == 0 and c == 0, q == PAIRS - 1, True)
                last.then_inc(y_mm, 1)

            def attend(n):
                pe.wait_ge(max_placed, 32 * (n + 1))
                pe.wait_ge(max_done, (n + 1) * H * C)
                pe.wait_ge(rowmaxT_ready, n + 1)
                wait(pe, out_ready, n)
                for step in range(H + LAG + 4):
                    if step < H:
                        scores(n, step)
                    if 0 <= step - LAG < H:
                        times_v(n, step - LAG)
                    if step - LAG - 1 >= 0 and (step - LAG - 1) % 2 == 1 and (step - LAG - 1) < H:
                        turn_heads(n, (step - LAG - 1) // 2)
                    if step - LAG - 2 >= 0 and (step - LAG - 2) % 2 == 1 and (step - LAG - 2) < H:
                        times_wo(n, (step - LAG - 2) // 2)

            def route(n):
                pe.wait_ge(exp_done, (n + 1) * H * UNITS)
                pe.wait_ge(h2_lo, n + 1)
                transpose_split(S0, split_hl).then_inc(h2T_mm, 1)
                pe.wait_ge(h2T_ready, n + 1)
                for c in range(C):
                    tok = slice(c * P, c * P + P)
                    last = product(S1[:, c * NE:(c + 1) * NE], h2T[:, 0, tok], h2T[:, 1, tok], wh(WG, 0, NE), wl(WG, 0, NE))
                last.then_inc(logit_mm, 1)
                pe.wait_ge(comb_split, 5 * n + 5)
                for c in range(C):
                    last = pe.transpose(half(S2)[:, c * P:c * P + P], comb_parts[:, c].rearrange("p a e -> p (a e)"), ident[:, :])
                last.then_inc(combT_mm, 1)

            def experts_up(n, j, last_projection):
                if j >= 2:
                    pe.wait_ge(sg_done, n * EP + j - 1)
                    pe.wait_ge(up_done, n * EP + j - 1)
                    pe.wait_ge(a32_done, n * EP + j - 1)
                product(gate_banks[j % 2][:, :], wh(WGU, j * 2 * P, P), wl(WGU, j * 2 * P, P), h2T[:, 0, :], h2T[:, 1, :]).then_inc(g_mm, 1)
                product(up_banks[j % 2][:, :], wh(WGU, j * 2 * P + P, P), wl(WGU, j * 2 * P + P, P),
                        h2T[:, 0, :], h2T[:, 1, :]).then_inc(u_mm, 1)
                mm(weight_banks[j % 2][:, :], select[:, j, :], combT[:, :], True, True).then_inc(wgt_mm, 1)

            def experts_down(n, j):
                pe.wait_ge(a_lo_done, n * EP + j + 1)
                for c in range(C):
                    tok = slice(c * P, c * P + P)
                    last = product(XB[:, c * P:c * P + P], a_hi[:, j % 3, tok], a_lo[:, j % 3, tok],
                                   wh(WD, j * D, D), wl(WD, j * D, D), j == 0 and c == 0, j == EP - 1, True)
                last.then_inc(down_mm, 1)

            def experts(n, projected):
                pe.wait_ge(combT_ready, n + 1)
                pe.wait_ge(logits_done, n + 1)
                if projected:
                    pe.wait_ge(proj_lo, (n + 2) * NPROJ)
                pe.wait_ge(y0_done, n + 1)
                for j in range(EP + LAG):
                    if j < EP:
                        experts_up(n, j, projected)
                    if j >= LAG:
                        experts_down(n, j - LAG)

            pe.wait_ge(consts_loaded, 80)
            pe.wait_ge(w_lo_done, 7)
            project(0)
            def sequence(n, more):
                row_maxima(n)
                attend(n)
                if more:
                    project(n + 1)
                route(n)
                experts(n, more)

            sequence(0, True)
            with pe.Fori(1, B - 1) as i:
                sequence(i, True)
            sequence(B - 1, False)

        @block.scalar
        def _(act):
            def project(n):
                act.wait_ge(hT_mm, n + 1)
                wait(act, proj_mm, n * NPROJ)
                act.activation(hT[:, :, :].rearrange("p a s -> p (a s)"), half(G0), ACT.Copy).then_inc(hT_ready, 1)
                wait(act, pv_mm, n * H)
                for k in range(NPROJ):
                    bank = proj_banks[k % 4]
                    act.wait_ge(proj_mm, n * NPROJ + k + 1)
                    if k < 8:
                        c, side = k // 2, k % 2
                        act.activation(v_hi[:, c, 8 * side:8 * side + 8, 0:E], bank[:, :].rearrange("p (h e) -> p h e", h=8),
                                       ACT.Copy).then_inc(proj_hi, 1)
                    else:
                        pair, w = (k - 8) // 2, k % 2
                        g = pair // 2
                        if pair % 2 == 0 and w == 0:
                            wait(act, placed[g - 2] if g >= 2 else placed[g + 2], 192 * (n + 1) if g >= 2 else 192 * n)
                        act.activation(nat_hi[:, g % 2, w, pair % 2, :], bank[:, :], ACT.Copy).then_inc(proj_hi, 1)

            def attend(n):
                act.wait_ge(rowmaxT_mm, n + 1)
                wait(act, max_placed, 32 * n)
                act.activation(rowmaxT[:, :], half(G0)[0:2 * H, 0:S], ACT.Copy).then_inc(rowmaxT_ready, 1)
                for step in range(H + LAG + 1):
                    if step < H:
                        for u, (at, cols) in enumerate(((0, 512), (512, 512), (1024, 256))):
                            act.wait_ge(score_mm, n * H * UNITS + step * UNITS + u + 1)
                            if u == 0:
                                used = max(0, step - 2)
                                wait(act, p_lo_dve, n * H + used)
                                wait(act, p_lo_pool, n * H + used)
                            act.activation(p32[:, step % 3, at:at + cols], score_banks[u][:, 0:cols], ACT.Exp,
                                           scale=back[:, SC_SCORE:SC_SCORE + 1]).then_inc(exp_done, 1)
                    h = step - LAG - 1
                    if 0 <= h < H:
                        q, ab = h // 2, h % 2
                        if ab == 0:
                            wait(act, oT_mm, n * PAIRS + max(0, q - 1))
                        act.wait_ge(o32_done, n * H + h + 1)
                        act.activation(o_hl[:, q % 2, 0, :, E * ab:E * ab + E], o32[:, h % 2], ACT.Copy).then_inc(o_hi_done, 1)
                    if h >= 2 and h % 2 == 0:
                        copy_oT(n, h // 2 - 1)
                copy_oT(n, PAIRS - 1)

            def copy_oT(n, q):
                act.wait_ge(oT_mm, n * PAIRS + q + 1)
                wait(act, y_mm, n * PAIRS + max(0, q - 1))
                act.activation(oT[:, q % 2].rearrange("p a s -> p (a s)"), half(oT_banks[q % 2]), ACT.Copy).then_inc(oT_ready, 1)

            def route(n):
                act.wait_ge(h2T_mm, n + 1)
                wait(act, u_mm, n * EP)
                act.activation(h2T[:, :, :].rearrange("p a s -> p (a s)"), half(S0), ACT.Copy).then_inc(h2T_ready, 1)
                act.wait_ge(shift_done, n + 1)
                wait(act, exm_done, n)
                act.activation(ex[:, :, :], shifted[:, :, :], ACT.Exp).then_inc(ex_done, 1)
                act.wait_ge(combT_mm, n + 1)
                wait(act, wgt_mm, n * EP)
                act.activation(combT[:, :], half(S2)[:, 0:S], ACT.Copy).then_inc(combT_ready, 1)

            def experts(n):
                def a_high(j):
                    act.wait_ge(a32_done, n * EP + j + 1)
                    wait(act, down_mm, n * EP + max(0, j - 2))
                    act.activation(a_hi[:, j % 3, :], a32[:, j % 2, :], ACT.Copy).then_inc(a_hi_done, 1)
                for j in range(EP):
                    act.wait_ge(g_mm, n * EP + j + 1)
                    wait(act, sg_done, n * EP + max(0, j - 1))
                    act.activation(th[:, j % 2, :], gate_banks[j % 2][:, :], ACT.Tanh, scale=back[:, SC_TANH:SC_TANH + 1]).then_inc(th_done, 1)
                    act.wait_ge(u_mm, n * EP + j + 1)
                    wait(act, su_done, n * EP + max(0, j - 1))
                    act.activation(up[:, j % 2, :], up_banks[j % 2][:, :], ACT.Copy).then_inc(up_done, 1)
                    if j >= 1:
                        a_high(j - 1)
                a_high(EP - 1)

            act.wait_ge(w_scaling, 8)
            project(0)
            def sequence(n, more):
                attend(n)
                if more:
                    project(n + 1)
                route(n)
                experts(n)

            sequence(0, True)
            with act.Fori(1, B - 1) as i:
                sequence(i, True)
            sequence(B - 1, False)

        @block.vector
        def _(dve):
            def norm_stats(n, which, src):
                wait(dve, ln_mv[which], C * n)
                for c in range(C):
                    dve.bn_stats(stats[:, which, c, :], src[:, c, :]).then_inc(ln_stats[which], 1)
                dve.wait_ge(ln_stats[which], C * (n + 1))
                wait(dve, ln_out[which], C * n)
                wait(dve, ln_var[which], n)
                apart(dve)
                for c in range(C):
                    dve.bn_aggr(mv[:, which, c, :], stats[:, which, c, :]).then_inc(ln_mv[which], 1)

            def norm_apply(n, which, src, dst):
                dve.wait_ge(ln_rstd[which], n + 1)
                for c in range(C):
                    dve.tensor_scalar(dst[:, c, :], src[:, c, :], mv[:, which, c, 0:1], rstd[:, which, c:c + 1],
                                      ALU.subtract, ALU.mult).then_inc(ln_out[which], 1)

            def split_norm(n, which, src, hl, hi_sem, lo_sem):
                dve.wait_ge(ln_out[which], C * (n + 1))
                dve.tensor_copy(hl[:, 0], src).then_inc(hi_sem, 1)
                dve.wait_ge(hi_sem, n + 1)
                dve.tensor_tensor(hl[:, 1], src, hl[:, 0], ALU.subtract).then_inc(lo_sem, 1)

            def normalise_input(n):
                dve.wait_ge(x_loaded, 16 * (n + 1))
                norm_stats(n, 0, xt)
                wait(dve, cur_copied, 2 * n)
                norm_apply(n, 0, xt, h32)
                wait(dve, h2T_mm, n - 1)
                split_norm(n, 0, h32[:, :, :], split_hl, h_hi, h_lo)

            def project_low(n):
                wait(dve, pv_mm, n * H)
                for k in range(NPROJ):
                    bank = proj_banks[k % 4]
                    dve.wait_ge(proj_hi, n * NPROJ + k + 1)
                    if k < 8:
                        c, side = k // 2, k % 2
                        dve.tensor_tensor(v_lo[:, c, 8 * side:8 * side + 8, :], bank[:, :].rearrange("p (h e) -> p h e", h=8),
                                          v_hi[:, c, 8 * side:8 * side + 8, 0:E], ALU.subtract).then_inc(proj_lo, 1)
                    else:
                        pair, w = (k - 8) // 2, k % 2
                        g = pair // 2
                        if pair % 2 == 0 and w == 0:
                            wait(dve, placed[g - 2] if g >= 2 else placed[g + 2], 192 * (n + 1) if g >= 2 else 192 * n)
                        dve.tensor_tensor(nat_lo[:, g % 2, w, pair % 2, :], bank[:, :], nat_hi[:, g % 2, w, pair % 2, :],
                                          ALU.subtract).then_inc(proj_lo, 1)

            def row_maxima(n):
                wait(dve, rowmax_lo, n)
                for h in range(H):
                    for c in range(C):
                        k = h * C + c
                        cols, hs = (c + 1) * P, (h % 2) * PAIRS + h // 2
                        dve.wait_ge(max_mm, n * H * C + k + 1)
                        wait(dve, max_done, n * H * C + max(0, k - 1))
                        apart(dve)
                        dve.tensor_tensor_reduce(max_junk[:, k % 2, 0:cols], score_banks[k % 3][:, 0:cols], mask[:, S - cols:S],
                                                 1.0, NEG, ALU.add, ALU.max, rowmax[:, c, hs:hs + 1]).then_inc(max_done, 1)
                dve.wait_ge(max_done, (n + 1) * H * C)
                wait(dve, rowmaxT_mm, n)
                dve.tensor_scalar(rowmax_hl[:, :, 0, :], rowmax[:, :, :], -1.0 / MAX_UNIT, None, ALU.mult).then_inc(rowmax_hi, 1)
                dve.wait_ge(rowmax_hi, n + 1)
                dve.scalar_tensor_tensor(rowmax_hl[:, :, 1, :], rowmax[:, :, :], -1.0 / MAX_UNIT, rowmax_hl[:, :, 0, :],
                                         ALU.mult, ALU.subtract).then_inc(rowmax_lo, 1)

            def attend(n):
                for step in range(H + LAG + 2):
                    h = step - 1
                    if 0 <= h < H:
                        dve.wait_ge(masked, n * H + h + 1)
                        wait(dve, pv_mm, n * H + max(0, h - 2))
                        dve.tensor_copy(p_hi[:, h % 3, :], p32[:, h % 3, :]).then_inc(p_hi_done, 1)
                        dve.wait_ge(p_hi_done, n * H + h + 1)
                        dve.tensor_tensor(p_lo[:, h % 3, 0:S], p32[:, h % 3, 0:S], p_hi[:, h % 3, 0:S], ALU.subtract).then_inc(p_lo_dve, 1)
                    h = step - LAG - 1
                    if 0 <= h < H:
                        q, ab = h // 2, h % 2
                        bank = pv_banks[h % 2][:, 0:C * (E + 1)].rearrange("p (c e) -> p c e", c=C)
                        dve.wait_ge(pv_mm, n * H + h + 1)
                        dve.reciprocal(rden[:, h % 2, :].rearrange("p (c a) -> p c a", a=1), bank[:, :, E:E + 1]).then_inc(rden_done, 1)
                        dve.wait_ge(rden_done, n * H + h + 1)
                        wait(dve, o_hi_done, n * H + max(0, h - 1))
                        wait(dve, o_lo_done, n * H + max(0, h - 1))
                        dve.tensor_tensor(o32[:, h % 2], bank[:, :, 0:E],
                                          rden[:, h % 2, :].rearrange("p (c a) -> p c a", a=1).to_broadcast([P, C, E]), ALU.mult).then_inc(o32_done, 1)
                        if h > 0:
                            low(n, h - 1)
                low(n, H - 1)

            def low(n, h):
                q, ab = h // 2, h % 2
                cols = slice(E * ab, E * ab + E)
                dve.wait_ge(o_hi_done, n * H + h + 1)
                wait(dve, oT_mm, n * PAIRS + max(0, q - 1))
                dve.tensor_tensor(o_hl[:, q % 2, 1, :, cols], o32[:, h % 2], o_hl[:, q % 2, 0, :, cols], ALU.subtract).then_inc(o_lo_done, 1)

            def residual(n, projected):
                dve.wait_ge(y_mm, PAIRS * (n + 1))
                dve.wait_ge(cur_copied, 2 * n + 2)
                wait(dve, out_stored, 16 * n)
                dve.scalar_tensor_tensor(y0[:, :, :], XB[:, :].rearrange("p (c d) -> p c d", c=C), back[:, SC_Y:SC_Y + 1],
                                         h_cur[:, :, :], ALU.mult, ALU.add).then_inc(y0_done, 1)
                dve.wait_ge(y0_done, n + 1)
                norm_stats(n, 1, y0)
                wait(dve, yg_done, n)
                norm_apply(n, 1, y0, y0)
                dve.wait_ge(ln_out[1], C * (n + 1))
                wait(dve, x1_done, n)
                dve.tensor_tensor(y0[:, :, :], y0[:, :, :], gam[:, :, :].to_broadcast([P, C, D]), ALU.mult).then_inc(yg_done, 1)
                dve.wait_ge(yg_done, n + 1)
                wait(dve, out_ready, n)
                dve.tensor_tensor(x1[:, :, :], y0[:, :, :], xb_cur[:, :, :], ALU.add).then_inc(x1_done, 1)
                dve.wait_ge(x1_done, n + 1)
                norm_stats(n, 2, x1)
                wait(dve, h2_lo, n)
                dve.wait_ge(x1_done, n + 1)
                norm_apply(n, 2, x1, y0)
                dve.wait_ge(hT_mm, n + 2 if projected else n + 1)
                split_norm(n, 2, y0[:, :, :], split_hl, h2_hi, h2_lo)

            def route(n):
                dve.wait_ge(logit_mm, n + 1)
                wait(dve, shift_done, n)
                wait(dve, chosen_done, n)
                dve.tensor_scalar(logits[:, :, :], S1[:, 0:C * NE].rearrange("p (c e) -> p c e", c=C), w_back[:, WG:WG + 1], None,
                                  ALU.mult).then_inc(logits_done, 1)
                dve.wait_ge(logits_done, n + 1)
                wait(dve, drop_done, C * n)
                apart(dve)
                for c in range(C):
                    dve.max(top8[:, c, :], logits[:, c, :]).then_inc(top_done, 1)
                dve.wait_ge(top_done, C * (n + 1))
                apart(dve)
                for c in range(C):
                    dve.match_replace(dropped[:, c, :], top8[:, c, :], logits[:, c, :], NEG).then_inc(drop_done, 1)
                wait(dve, ex_done, n)
                dve.tensor_tensor(shifted[:, :, :], logits[:, :, :], top8[:, :, 0:1].to_broadcast([P, C, NE]), ALU.subtract).then_inc(shift_done, 1)
                dve.wait_ge(drop_done, C * (n + 1))
                wait(dve, exm_done, n)
                dve.tensor_tensor(chosen[:, :, :], dropped[:, :, :], logits[:, :, :], ALU.not_equal).then_inc(chosen_done, 1)
                dve.wait_ge(chosen_done, n + 1)
                dve.wait_ge(ex_done, n + 1)
                wait(dve, comb_done, n)
                dve.tensor_tensor(exm[:, :, :], ex[:, :, :], chosen[:, :, :], ALU.mult).then_inc(exm_done, 1)
                dve.wait_ge(exm_done, n + 1)
                wait(dve, exinv_done, n)
                dve.tensor_reduce(exsum[:, :], exm[:, :, :], AX.X, ALU.add).then_inc(exsum_done, 1)
                dve.wait_ge(exsum_done, n + 1)
                dve.reciprocal(exinv[:, :], exsum[:, :]).then_inc(exinv_done, 1)
                dve.wait_ge(exinv_done, n + 1)
                wait(dve, comb_split, 5 * n)
                wait(dve, combT_mm, n)
                dve.tensor_tensor(comb[:, :, :], exm[:, :, :], exinv[:, :].rearrange("p (c a) -> p c a", a=1).to_broadcast([P, C, NE]),
                                  ALU.mult).then_inc(comb_done, 1)
                dve.wait_ge(comb_done, n + 1)
                dve.tensor_copy(comb_parts[:, :, 0, :], comb[:, :, :]).then_inc(comb_split, 1)
                dve.wait_ge(comb_split, 5 * n + 1)
                dve.tensor_tensor(comb_rest[:, :, :], comb[:, :, :], comb_parts[:, :, 0, :], ALU.subtract).then_inc(comb_split, 1)
                dve.wait_ge(comb_split, 5 * n + 2)
                dve.tensor_copy(comb_parts[:, :, 1, :], comb_rest[:, :, :]).then_inc(comb_split, 1)
                dve.wait_ge(comb_split, 5 * n + 3)
                dve.tensor_tensor(comb_parts[:, :, 2, :], comb_rest[:, :, :], comb_parts[:, :, 1, :], ALU.subtract).then_inc(comb_split, 2)

            def experts(n):
                def finish(j):
                    dve.wait_ge(su_done, n * EP + j + 1)
                    dve.wait_ge(wgt_mm, n * EP + j + 1)
                    wait(dve, a_hi_done, n * EP + max(0, j - 1))
                    wait(dve, a_lo_done, n * EP + max(0, j - 1))
                    dve.tensor_tensor(a32[:, j % 2, :], weight_banks[j % 2][:, :], su[:, j % 2, :], ALU.mult).then_inc(a32_done, 1)

                def a_low(j):
                    dve.wait_ge(a_hi_done, n * EP + j + 1)
                    wait(dve, down_mm, n * EP + max(0, j - 2))
                    dve.tensor_tensor(a_lo[:, j % 3, :], a32[:, j % 2, :], a_hi[:, j % 3, :], ALU.subtract).then_inc(a_lo_done, 1)
                for j in range(EP + 2):
                    if j < EP:
                        dve.wait_ge(th_done, n * EP + j + 1)
                        wait(dve, su_done, n * EP + max(0, j - 1))
                        dve.scalar_tensor_tensor(sg[:, j % 2, :], th[:, j % 2, :], 1.0, gate_banks[j % 2][:, :], ALU.add, ALU.mult).then_inc(sg_done, 1)
                    if 1 <= j <= EP:
                        finish(j - 1)
                    if j >= 2:
                        a_low(j - 2)
                dve.wait_ge(down_mm, EP * (n + 1))
                dve.wait_ge(h2_lo, n + 1)
                dve.scalar_tensor_tensor(y0[:, :, :], XB[:, :].rearrange("p (c d) -> p c d", c=C), back[:, SC_OUT:SC_OUT + 1],
                                         x1[:, :, :], ALU.mult, ALU.add).then_inc(out_ready, 1)

            dve.memset(w_absmax[:, :], 1.0).then_inc(consts_set, 1)
            dve.wait_ge(consts_set, 1)
            for w in range(7):
                dve.wait_ge(w_loaded, 16 * 7)
                dve.tensor_reduce(w_absmax[:, w:w + 1], raw[:, WAT[w]:WAT[w] + WCOLS[w]], AX.X, ALU.max,
                                  apply_absolute_value=True).then_inc(w_maxed, 1)
            dve.wait_ge(w_allmaxed, 1)
            dve.tensor_scalar(w_allmax[:, :], w_allmax[:, :], 2.0 ** -100, None, ALU.max).then_inc(w_scaling, 1)
            dve.wait_ge(w_scaling, 1)
            dve.tensor_scalar(w_pow[:, :].bitcast(I32), w_allmax[:, :].bitcast(I32), 0x7F800000, None, ALU.bitwise_and).then_inc(w_scaling, 1)
            dve.wait_ge(w_scaling, 2)
            dve.tensor_scalar(w_back[:, :], w_pow[:, :], 0.125, None, ALU.mult).then_inc(w_scaling, 1)
            dve.wait_ge(w_scaling, 3)
            dve.reciprocal(w_scale[:, :], w_back[:, :]).then_inc(w_scaling, 1)

            def pair_product(dst, a, b, factor):
                return dve.scalar_tensor_tensor(back[:, dst:dst + 1], a, factor, b, ALU.mult, ALU.mult)

            def wb(w):
                return w_back[:, w:w + 1]
            pair_product(SC_SCORE, wb(WQ), wb(WK), float(E) ** -0.5).then_inc(w_scaling, 1)
            pair_product(SC_Y, wb(WV), wb(WO), 1.0).then_inc(w_scaling, 1)
            pair_product(SC_GU2, wb(WGU), wb(WGU), 0.5 / COMB_SHIFT).then_inc(w_scaling, 1)
            dve.tensor_scalar(back[:, SC_TANH:SC_TANH + 1], wb(WGU), 0.5, None, ALU.mult).then_inc(w_scaling, 1)
            dve.wait_ge(w_scaling, 8)
            pair_product(SC_OUT, back[:, SC_GU2:SC_GU2 + 1], wb(WD), 1.0).then_inc(w_scaling, 1)
            for w in range(7):
                src = raw[:, WAT[w]:WAT[w] + WCOLS[w]]
                scale = w_scale[:, w:w + 1]
                dve.tensor_scalar(wh(w, 0, WCOLS[w]), src, scale, None, ALU.mult).then_inc(w_hi_done, 1)
                dve.wait_ge(w_hi_done, w + 1)
                dve.scalar_tensor_tensor(wl(w, 0, WCOLS[w]), src, scale, wh(w, 0, WCOLS[w]), ALU.mult, ALU.subtract).then_inc(w_lo_done, 1)
            dve.wait_ge(w_lo_done, 7)
            dve.memset(KB[E:P].rearrange("p a b s -> p (a b s)").bitcast(F32), 0.0).then_inc(consts_set, 1)
            dve.memset(QB[E:P].rearrange("p a b s -> p (a b s)").bitcast(F32), 0.0).then_inc(consts_set, 1)
            dve.wait_ge(consts_set, 3)
            dve.memset(KB[E:E + 2].rearrange("p a b s -> p (a b s)"), MAX_UNIT).then_inc(consts_set, 1)
            dve.memset(v_hi[:, :, :, E:E + 1], 1.0).then_inc(consts_set, 1)
            dve.memset(comb_parts[:, :, 3, :], 0.0).then_inc(consts_set, 1)
            dve.wait_ge(consts_set, 6)
            dve.wait_ge(consts_loaded, 80)

            normalise_input(0)
            project_low(0)
            def sequence(n, more):
                row_maxima(n)
                if more:
                    normalise_input(n + 1)
                attend(n)
                residual(n, more)
                if more:
                    project_low(n + 1)
                route(n)
                experts(n)

            sequence(0, True)
            with dve.Fori(1, B - 1) as i:
                sequence(i, True)
            sequence(B - 1, False)

        @block.gpsimd
        def _(pool):
            def inverse_deviation(n, which, eps):
                pool.wait_ge(ln_mv[which], C * (n + 1))
                apart(pool)
                pool.tensor_scalar(var_eps[:, which, :].rearrange("p (c a) -> p c a", a=1), mv[:, which, :, 1:2], eps, 0.0, ALU.add, ALU.add).then_inc(ln_var[which], 1)
                pool.wait_ge(ln_var[which], n + 1)
                wait(pool, ln_out[which], C * n)
                pool.tensor_tensor(rstd[:, which, :], var_eps[:, which, :], minus_half[:, :], ALU.pow).then_inc(ln_rstd[which], 1)

            def normalise_input(n):
                inverse_deviation(n, 0, LN_EPS)

            def keep_current(n):
                pool.wait_ge(h_lo, n + 1)
                wait(pool, x1_done, n)
                apart(pool)
                pool.tensor_copy(h_cur[:, :, :], h32[:, :, :]).then_inc(cur_copied, 1)
                pool.wait_ge(x_loaded, 16 * (n + 1))
                pool.tensor_tensor(xb_cur[:, :, :], xt[:, :, :], bet[:, :, :].to_broadcast([P, C, D]), ALU.add).then_inc(cur_copied, 1)

            def attend(n):
                for step in range(H + 1):
                    if step < H:
                        pool.wait_ge(exp_done, n * H * UNITS + UNITS * (step + 1))
                        apart(pool)
                        p = p32[:, step % 3, :]
                        keep = dict(compare_op=ALU.is_ge, fill=0.0, base=0, channel_multiplier=-1)
                        far = p[:, 0:1024].rearrange("p (a s) -> p a s", a=2)[:, :, 0:P]
                        pool.affine_select(far, far, pattern=[[0, 2], [1, P]], **keep).then_inc(diag_pair, 1)
                        near = p[:, 896:1152].rearrange("p (a s) -> p a s", a=2)
                        pool.affine_select(near, near, pattern=[[0, 2], [1, P]], **keep).then_inc(masked, 1)
                    h = step - 1
                    if h >= 0:
                        pool.wait_ge(p_hi_done, n * H + h + 1)
                        wait(pool, pv_mm, n * H + max(0, h - 2))
                        pool.tensor_tensor(p_lo[:, h % 3, S:PCOLS], p32[:, h % 3, S:PCOLS], p_hi[:, h % 3, S:PCOLS], ALU.subtract).then_inc(p_lo_pool, 1)

            def experts(n):
                for j in range(EP):
                    pool.wait_ge(up_done, n * EP + j + 1)
                    pool.wait_ge(sg_done, n * EP + j + 1)
                    wait(pool, a32_done, n * EP + max(0, j - 1))
                    pool.tensor_tensor(su[:, j % 2, :], sg[:, j % 2, :], up[:, j % 2, :], ALU.mult).then_inc(su_done, 1)

            pool.memset(minus_half[:, :], -0.5).then_inc(pool_set, 1)
            pool.wait_ge(w_maxed, 7)
            pool.partition_all_reduce(w_allmax[:, :], w_absmax[:, :], P, bass.bass_isa.ReduceOp.absmax).then_inc(w_allmaxed, 1)
            pool.wait_ge(pool_set, 1)
            pool.wait_ge(consts_loaded, 80)
            normalise_input(0)
            def sequence(n, more):
                keep_current(n)
                if more:
                    normalise_input(n + 1)
                attend(n)
                inverse_deviation(n, 1, ATTN_LN_EPS)
                inverse_deviation(n, 2, LN_EPS)
                experts(n)

            sequence(0, True)
            with pool.Fori(1, B - 1) as i:
                sequence(i, True)
            sequence(B - 1, False)


_INS = ("L0_attn_x", "L0_attn_Wq", "L0_attn_Wk", "L0_attn_Wv", "L0_attn_Wo", "L0_attn_gamma", "L0_attn_beta",
        "L0_ffn_gate_w", "L0_ffn_gate_up_w", "L0_ffn_down_w")


def kernel(**inputs):
    import concourse.bacc as bacc
    from concourse.bass_utils import run_bass_kernel_spmd

    x, wq, wk, wv, wo, gamma, beta, gate_w, gate_up_w, down_w = (np.asarray(inputs[n]) for n in _INS)
    cont = np.ascontiguousarray

    def by_width(w):
        return cont(w.transpose(1, 0, 2).reshape(D, H * E))
    gu = gate_up_w.reshape(EP, 2, 2, ED, D).transpose(4, 0, 2, 1, 3)
    select = np.zeros((P, EP, P), np.float16)
    for part in range(3):
        for e in range(NE):
            select[part * NE + e, e // 2, (e % 2) * ED:(e % 2) * ED + ED] = COMB_SHIFT
    col = np.arange(S) - (S - P)
    arrays = {
        "x": cont(x), "wq": by_width(wq), "wk": by_width(wk), "wv": by_width(wv),
        "wo": cont(wo.reshape(PAIRS, P, D).transpose(1, 0, 2).reshape(P, PAIRS * D)),
        "gamma": cont(np.broadcast_to(gamma, (P, 1, D))), "beta": cont(np.broadcast_to(beta, (P, 1, D))),
        "gate": cont(gate_w.T), "gate_up": cont(gu.reshape(D, EP * 4 * ED)),
        "down": cont(down_w.reshape(EP, 2, D, ED).transpose(1, 3, 0, 2).reshape(P, EP * D)),
        "ident": np.eye(P, dtype=np.float16),
        "mask": np.where(col[None, :] > np.arange(P)[:, None], np.float32(NEG), np.float32(0.0)),
        "select": select,
    }
    nc = bacc.Bacc("TRN2", target_bir_lowering=False, num_devices=1)
    args = [nc.dram_tensor(f"in_{n}", a.shape, mybir.dt.from_np(a.dtype), kind="ExternalInput").ap() for n, a in arrays.items()]
    out = nc.dram_tensor("out_y", (B, S, D), F32, kind="ExternalOutput").ap()
    layer(nc, *args, out)
    r = run_bass_kernel_spmd(nc, [{f"in_{n}": a for n, a in arrays.items()}], core_ids=[0])
    return r.results[0]["out_y"]
```

```python
from contextlib import ExitStack

import numpy as np
import concourse.bass as bass
from concourse import mybir

F32, F16, I32 = mybir.dt.float32, mybir.dt.float16, mybir.dt.int32
ALU = mybir.AluOpType
ACT = mybir.ActivationFunctionType
AX = mybir.AxisListType

P = 128
B, S, D = 16, 512, 128
H, E = 16, 64
PAIRS = H // 2
C = S // P
NE, TOPK, ED = 32, 8, 64
EP = NE // 2
GROUPS = 4
LN_EPS, ATTN_LN_EPS = 1e-5, 1e-3
MAX_UNIT = 2.0 ** 13
COMB_SHIFT = 2.0 ** -8
NEG = -3.0e38
LAG = 3
TURN = 6
DOWN_LAG = 3
UNITS = 3
PCOLS = 1280
NPROJ = 8 + 2 * PAIRS
TURN_AT = 10
LOGITS_AT = 14
EXP_AT = 14
SPREAD_AT = 20
NORM_AT = (2, 4)
CHOOSE_AT = 12
WEIGH_AT = 16


def prob_col(t, c):
    return {0: c * P, 1: 512 + (c - 1) * P, 2: 1024 + (c - 2) * P, 3: 896}[t]


def layer(nc, x, wq, wk, wv, wo, gamma, beta, gate, gate_up, down, ident_c, mask_c, select_c, out):
    with ExitStack() as ctx:
        def sb(name, shape, dt):
            return ctx.enter_context(nc.sbuf_tensor(name, shape, dt))

        def sem(name):
            return ctx.enter_context(nc.semaphore(name))

        ident = sb("ident", [P, P], F16)
        mask = sb("mask", [P, S], F32)
        select = sb("select", [P, EP, P], F16)
        score_ops = sb("score_ops", [P, 4, 2, PAIRS, S], F16)
        KA, KB, QA, QB = (score_ops[:, n] for n in range(4))
        raw = score_ops[:, :, :, :, :].rearrange("p a b c d -> p (a b c d)").bitcast(F32)
        WCOLS = [D * 8, D * 8, D * 8, D * 8, EP * 2 * P, EP * D, NE]
        WQ, WK, WV, WO, WGU, WD, WG = range(7)
        WAT = [sum(WCOLS[:n]) for n in range(7)]
        w_hi = sb("w_hi", [P, sum(WCOLS)], F16)
        w_lo = sb("w_lo", [P, sum(WCOLS)], F16)
        w_absmax = sb("w_absmax", [P, 8], F32)
        w_allmax = sb("w_allmax", [P, 8], F32)
        w_pow = sb("w_pow", [P, 8], F32)
        w_scale = sb("w_scale", [P, 8], F32)
        w_back = sb("w_back", [P, 8], F32)
        back = sb("back", [P, 8], F32)
        SC_SCORE, SC_Y, SC_TANH, SC_OUT, SC_GU2 = range(5)
        gam = sb("gam", [P, 1, D], F32)
        bet = sb("bet", [P, 1, D], F32)
        minus_half = sb("minus_half", [P, C], F32)

        xt = sb("xt", [P, C, D], F32)
        h32 = sb("h32", [P, C, D], F32)
        h_cur = sb("h_cur", [P, C, D], F32)
        xb_cur = sb("xb_cur", [P, C, D], F32)
        split_hl = sb("split_hl", [P, 2, C, D], F16)
        hT = sb("hT", [P, 2, S], F16)
        stats = sb("stats", [P, 3, C, 6], F32)
        mv = sb("mv", [P, 3, C, 2], F32)
        var_eps = sb("var_eps", [P, 3, C], F32)
        rstd = sb("rstd", [P, 3, C], F32)
        nat_hi = sb("nat_hi", [P, 2, 2, 2, S], F16)
        nat_lo = sb("nat_lo", [P, 2, 2, 2, S], F16)
        v_hi = sb("v_hi", [P, C, H, E + 1], F16)
        v_lo = sb("v_lo", [P, C, H, E], F16)
        max_junk = sb("max_junk", [P, 2, S], F16)
        rowmax = sb("rowmax", [P, C, H], F32)
        rowmax_hl = sb("rowmax_hl", [P, C, 2, H], F16)
        room = sb("room", [P, 6 * PCOLS], F32)

        def carve(at, slots, cols, dt):
            words = slots * cols // (1 if dt is F32 else 2)
            return room[:, at:at + words].bitcast(dt).rearrange("p (a b) -> p a b", a=slots)
        p32 = carve(0, 3, PCOLS, F32)
        p_hi, p_lo = (carve(at, 3, PCOLS, F16) for at in (3 * PCOLS, 3 * PCOLS + 3 * PCOLS // 2))
        th, sg = (carve(2 * S * n, 2, S, F32) for n in range(2))
        up, a32 = (carve(4 * S + 3 * S * n, 3, S, F32) for n in range(2))
        a_hi, a_lo = (carve(10 * S + n * 3 * S // 2, 3, S, F16) for n in range(2))
        logits, dropped, chosen, shifted, ex, exm, comb, comb_rest = (
            carve(13 * S + n * C * NE, C, NE, F32) for n in range(8))
        rden = sb("rden", [P, 2, C], F32)
        o32 = sb("o32", [P, 2, C, E], F32)
        o_hl = sb("o_hl", [P, 2, 2, C, 2 * E], F16)
        oT = sb("oT", [P, 2, 2, S], F16)
        y0 = sb("y0", [P, C, D], F32)
        x1 = sb("x1", [P, C, D], F32)
        h2T = sb("h2T", [P, 2, S], F16)
        top8 = sb("top8", [P, C, TOPK], F32)
        exsum = sb("exsum", [P, C], F32)
        exinv = sb("exinv", [P, C], F32)
        comb_parts = sb("comb_parts", [P, C, 4, NE], F16)
        combT = sb("combT", [P, S], F16)
        rowmaxT = combT[0:2 * H, :]

        S0, S1, S2, P0, P1, G0, G1, XB = (
            ctx.enter_context(nc.psum_tensor(f"bank_{n}", [P, S], F32)) for n in ("s0", "s1", "s2", "p0", "p1", "g0", "g1", "x"))
        score_banks = [S0, S1, S2]
        pv_banks = [P0, P1]
        proj_banks = [G0, G1, P0, P1]
        oT_banks = [G0, G1]
        gate_banks, up_banks, weight_bank = [S0, S1], [S2, P0], P1
        max_banks = [G0, G1]

        def half(bank):
            return bank[:, :].bitcast(F16)

        waits_met = sem("waits_met")
        consts_loaded = sem("consts_loaded")
        w_loaded = sem("w_loaded")
        w_maxed = sem("w_maxed")
        w_allmaxed = sem("w_allmaxed")
        w_scaling = sem("w_scaling")
        w_scaled = sem("w_scaled")
        w_hi_done = sem("w_hi_done")
        w_lo_done = sem("w_lo_done")
        consts_set = sem("consts_set")
        pool_set = sem("pool_set")
        x_loaded, cur_copied = sem("x_loaded"), sem("cur_copied")
        diag_pair = sem("diag_pair")
        ln_stats = [sem(f"ln{n}_stats") for n in range(3)]
        ln_mv = [sem(f"ln{n}_mv") for n in range(3)]
        ln_var = [sem(f"ln{n}_var") for n in range(3)]
        ln_rstd = [sem(f"ln{n}_rstd") for n in range(3)]
        ln_out = [sem(f"ln{n}_out") for n in range(3)]
        h_hi, h_lo = sem("h_hi"), sem("h_lo")
        hT_mm, hT_ready = sem("hT_mm"), sem("hT_ready")
        proj_mm, proj_hi, proj_lo = sem("proj_mm"), sem("proj_hi"), sem("proj_lo")
        placed = [sem(f"placed{g}") for g in range(GROUPS)]
        max_mm, max_done = sem("max_mm"), sem("max_done")
        rowmax_hi, rowmax_lo = sem("rowmax_hi"), sem("rowmax_lo")
        rowmaxT_mm, rowmaxT_ready, max_placed = sem("rowmaxT_mm"), sem("rowmaxT_ready"), sem("max_placed")
        score_mm, exp_done, masked = sem("score_mm"), sem("exp_done"), sem("masked")
        p_hi_done, p_lo_dve, p_lo_pool = sem("p_hi_done"), sem("p_lo_dve"), sem("p_lo_pool")
        pv_mm, rden_done, o32_done = sem("pv_mm"), sem("rden_done"), sem("o32_done")
        o_hi_done, o_lo_done = sem("o_hi_done"), sem("o_lo_done")
        oT_mm, oT_ready, y_mm = sem("oT_mm"), sem("oT_ready"), sem("y_mm")
        y0_done, yg_done, x1_done = sem("y0_done"), sem("yg_done"), sem("x1_done")
        h2_hi, h2_lo, h2T_mm, h2T_ready = sem("h2_hi"), sem("h2_lo"), sem("h2T_mm"), sem("h2T_ready")
        logit_mm, logits_done, top_done = sem("logit_mm"), sem("logits_done"), sem("top_done")
        drop_done, chosen_done, shift_done = sem("drop_done"), sem("chosen_done"), sem("shift_done")
        ex_done, exm_done, exsum_done, exinv_done = sem("ex_done"), sem("exm_done"), sem("exsum_done"), sem("exinv_done")
        comb_done, comb_split = sem("comb_done"), sem("comb_split")
        combT_mm, combT_ready = sem("combT_mm"), sem("combT_ready")
        g_mm, u_mm, wgt_mm = sem("g_mm"), sem("u_mm"), sem("wgt_mm")
        th_done, up_done, sg_done, su_done = sem("th_done"), sem("up_done"), sem("sg_done"), sem("su_done")
        a32_done, a_hi_done, a_lo_done, down_mm = sem("a32_done"), sem("a_hi_done"), sem("a_lo_done"), sem("down_mm")
        out_ready, out_stored = sem("out_ready"), sem("out_stored")

        def wh(w, a, n):
            return w_hi[:, WAT[w] + a:WAT[w] + a + n]

        def wl(w, a, n):
            return w_lo[:, WAT[w] + a:WAT[w] + a + n]

        def wait(eng, s, value):
            if not (isinstance(value, int) and value <= 0):
                eng.wait_ge(s, value)

        def apart(eng):
            eng.sem_inc(waits_met, 1)

        block = ctx.enter_context(nc.Block())

        @block.sync
        def _(sp):
            sp.dma_start(ident[:, :], ident_c).then_inc(consts_loaded, 16)
            sp.dma_start(mask[:, :], mask_c).then_inc(consts_loaded, 16)
            sp.dma_start(select[:, :, :], select_c).then_inc(consts_loaded, 16)
            sp.dma_start(gam[:, :, :], gamma).then_inc(consts_loaded, 16)
            sp.dma_start(bet[:, :, :], beta).then_inc(consts_loaded, 16)
            for w, src in enumerate((wq, wk, wv, wo, gate_up, down, gate)):
                sp.dma_start(raw[:, WAT[w]:WAT[w] + WCOLS[w]], src).then_inc(w_loaded, 16)

            def load_x(n):
                wait(sp, ln_out[0], C * n)
                apart(sp)
                wait(sp, cur_copied, 2 * n)
                apart(sp)
                sp.dma_start(xt[:, :, :], x[bass.ds(n, 1)].rearrange("a (c p) d -> p (a c) d", p=P)).then_inc(x_loaded, 16)

            def place_qk(n):
                wait(sp, score_mm, n * UNITS * H)
                sp.wait_ge(w_lo_done, 7)
                sp.wait_ge(consts_set, 6)
                for g in range(GROUPS):
                    done = n * NPROJ + 8 + 4 * (g + 1)
                    sp.wait_ge(proj_hi, done)
                    sp.wait_ge(proj_lo, done)
                    for ab in range(2):
                        rows = slice(E * ab, E * ab + E)
                        to = slice(2 * g, 2 * g + 2)
                        k_h, q_h = nat_hi[rows, g % 2, 0], nat_hi[rows, g % 2, 1]
                        k_l, q_l = nat_lo[rows, g % 2, 0], nat_lo[rows, g % 2, 1]
                        for dst, lower, src in ((KA, 0, k_h), (KA, 1, k_l), (KB, 0, k_h), (QA, 0, q_h), (QA, 1, q_h), (QB, 0, q_l)):
                            sp.dma_start(dst[E * lower:E * lower + E, ab, to, :], src).then_inc(placed[g], 16)

            def place_max(n):
                sp.wait_ge(rowmaxT_ready, n + 1)
                for part in range(2):
                    sp.dma_start(QB[E + part:E + part + 1].rearrange("a b p s -> a (b p) s"),
                                 rowmaxT[H * part:H * part + H, :]).then_inc(max_placed, 16)

            def store(n):
                sp.wait_ge(out_ready, n + 1)
                apart(sp)
                sp.dma_start(out[bass.ds(n, 1)].rearrange("a (c p) d -> p (a c) d", p=P), y0[:, :, :]).then_inc(out_stored, 16)

            load_x(0)
            place_qk(0)
            load_x(1)
            place_max(0)
            with sp.Fori(1, B - 1) as i:
                place_qk(i)
                load_x(i + 1)
                store(i - 1)
                place_max(i)
            place_qk(B - 1)
            store(B - 2)
            place_max(B - 1)
            store(B - 1)
            sp.wait_ge(out_stored, 16 * B)

        @block.tensor
        def _(pe):
            def mm(dst, lhsT, rhs, start, stop, shared=False):
                return pe.matmul(dst, lhsT, rhs, start=start, stop=stop, skip_group_check=shared)

            def product(dst, l_hi, l_lo, r_hi, r_lo, start=True, stop=True, shared=False):
                mm(dst, l_hi, r_hi, start, False, shared)
                mm(dst, l_hi, r_lo, False, False, shared)
                return mm(dst, l_lo, r_hi, False, stop, shared)

            def transpose_split(dst, hi_lo):
                for part in range(2):
                    for c in range(C):
                        last = pe.transpose(half(dst)[:, part * S + c * P:part * S + c * P + P], hi_lo[:, part, c, :], ident[:, :])
                return last

            def project(n):
                wait(pe, oT_ready, n * PAIRS)
                pe.wait_ge(h_lo, n + 1)
                transpose_split(G0, split_hl).then_inc(hT_mm, 1)
                pe.wait_ge(hT_ready, n + 1)
                wait(pe, o32_done, n * H)

            def project_units(n, first, end):
                for k in range(first, end):
                    bank = proj_banks[k % 4]
                    if k >= 4:
                        pe.wait_ge(proj_lo, n * NPROJ + k - 3)
                    if k < 8:
                        c, side = k // 2, k % 2
                        hc = slice(c * P, c * P + P)
                        last = product(bank[:, :], hT[:, 0, hc], hT[:, 1, hc], wh(WV, side * S, S), wl(WV, side * S, S))
                    else:
                        pair, w = (k - 8) // 2, (WK, WQ)[k % 2]
                        last = product(bank[:, :], wh(w, pair * P, P), wl(w, pair * P, P), hT[:, 0, :], hT[:, 1, :])
                    last.then_inc(proj_mm, 1)

            def max_scores(n, h, c):
                k, pair, ab, cols = h * C + c, h // 2, h % 2, (c + 1) * P
                if h % 4 == 0 and c == 0:
                    pe.wait_ge(placed[h // 4], 192 * (n + 1))
                if k >= 2:
                    pe.wait_ge(max_done, n * H * C + k - 1)
                mm(max_banks[k % 2][:, 0:cols], QA[:, ab, pair, c * P:c * P + P], KA[:, ab, pair, 0:cols],
                   True, True).then_inc(max_mm, 1)

            def turn_maxima(n):
                pe.wait_ge(rowmax_lo, n + 1)
                for c in range(C):
                    last = pe.transpose(half(G0)[0:2 * H, c * P:c * P + P],
                                        rowmax_hl[:, c].rearrange("p a h -> p (a h)"), ident[:, :])
                last.then_inc(rowmaxT_mm, 1)

            def scores(n, h):
                pair, ab = h // 2, h % 2
                for u, chunks in enumerate(((0,), (1, 3), (2,))):
                    k = h * UNITS + u
                    if k >= UNITS:
                        pe.wait_ge(exp_done, n * H * UNITS + k - 2)
                    for t in chunks:
                        cols, at = S - t * P, (384 if t == 3 else 0)
                        dst = score_banks[u][:, at:at + cols]
                        keys = slice(t * P, t * P + P)
                        mm(dst, KA[:, ab, pair, keys], QA[:, ab, pair, t * P:S], True, False)
                        last = mm(dst, KB[:, ab, pair, keys], QB[:, ab, pair, t * P:S], False, True)
                    last.then_inc(score_mm, 1)

            def times_v(n, h):
                if h >= 2:
                    pe.wait_ge(o32_done, n * H + h - 1)
                pe.wait_ge(p_lo_dve, n * H + h + 1)
                pe.wait_ge(p_lo_pool, n * H + h + 1)
                bank = pv_banks[h % 2]
                for c in range(C):
                    dst = bank[:, c * (E + 1):(c + 1) * (E + 1)]
                    for t in range(c + 1):
                        at = prob_col(t, c)
                        ph, pl = p_hi[:, h % 3, at:at + P], p_lo[:, h % 3, at:at + P]
                        mm(dst, ph, v_hi[:, t, h, :], t == 0, False)
                        mm(dst[:, 0:E], ph, v_lo[:, t, h, :], False, False)
                        last = mm(dst, pl, v_hi[:, t, h, :], False, t == c)
                last.then_inc(pv_mm, 1)

            def turn_heads(n, q):
                if q >= 2:
                    pe.wait_ge(oT_ready, n * PAIRS + q - 1)
                pe.wait_ge(o_lo_done, n * H + 2 * q + 2)
                pe.wait_ge(o_hi_done, n * H + 2 * q + 2)
                transpose_split(oT_banks[q % 2], o_hl[:, q % 2]).then_inc(oT_mm, 1)

            def times_wo(n, q):
                pe.wait_ge(oT_ready, n * PAIRS + q + 1)
                for c in range(C):
                    tok = slice(c * P, c * P + P)
                    last = product(XB[:, c * P:c * P + P], oT[:, q % 2, 0, tok], oT[:, q % 2, 1, tok],
                                   wh(WO, q * P, P), wl(WO, q * P, P), q == 0 and c == 0, q == PAIRS - 1, True)
                last.then_inc(y_mm, 1)

            def attend(n):
                pe.wait_ge(max_placed, 32 * (n + 1))
                wait(pe, sg_done, n * EP)
                wait(pe, up_done, n * EP)
                wait(pe, a32_done, n * EP)
                pe.wait_ge(rowmaxT_ready, n + 1)
                wait(pe, out_ready, n)
                for step in range(H + TURN + 1):
                    if step < H:
                        scores(n, step)
                    if 0 <= step - LAG < H:
                        times_v(n, step - LAG)
                    h = step - TURN
                    if 0 <= h < H and h % 2 == 1:
                        turn_heads(n, h // 2)
                    if 0 <= h - 1 < H and h % 2 == 0:
                        times_wo(n, (h - 1) // 2)

            def route(n, more):
                def projections(first, end):
                    if more:
                        project_units(n + 1, first, end)
                if more:
                    project(n + 1)
                projections(0, TURN_AT)
                pe.wait_ge(exp_done, (n + 1) * H * UNITS)
                pe.wait_ge(h2_lo, n + 1)
                transpose_split(S0, split_hl).then_inc(h2T_mm, 1)
                projections(TURN_AT, LOGITS_AT)
                pe.wait_ge(h2T_ready, n + 1)
                for c in range(C):
                    tok = slice(c * P, c * P + P)
                    last = product(S1[:, c * NE:(c + 1) * NE], h2T[:, 0, tok], h2T[:, 1, tok], wh(WG, 0, NE), wl(WG, 0, NE))
                last.then_inc(logit_mm, 1)
                projections(LOGITS_AT, SPREAD_AT)
                pe.wait_ge(comb_split, 5 * n + 5)
                for c in range(C):
                    last = pe.transpose(half(S2)[:, c * P:c * P + P], comb_parts[:, c].rearrange("p a e -> p (a e)"), ident[:, :])
                last.then_inc(combT_mm, 1)
                projections(SPREAD_AT, NPROJ)

            def gate(n, j):
                if j >= 2:
                    pe.wait_ge(sg_done, n * EP + j - 1)
                product(gate_banks[j % 2][:, :], wh(WGU, j * 2 * P, P), wl(WGU, j * 2 * P, P), h2T[:, 0, :], h2T[:, 1, :]).then_inc(g_mm, 1)

            def up_product(n, j):
                if j >= 2:
                    pe.wait_ge(up_done, n * EP + j - 1)
                product(up_banks[j % 2][:, :], wh(WGU, j * 2 * P + P, P), wl(WGU, j * 2 * P + P, P),
                        h2T[:, 0, :], h2T[:, 1, :]).then_inc(u_mm, 1)

            def spread_weights(n, j):
                if j >= 1:
                    pe.wait_ge(a32_done, n * EP + j)
                mm(weight_bank[:, :], select[:, j, :], combT[:, :], True, True).then_inc(wgt_mm, 1)

            def experts_down(n, j):
                pe.wait_ge(a_lo_done, n * EP + j + 1)
                if j == 0:
                    pe.wait_ge(y0_done, n + 1)
                for c in range(C):
                    tok = slice(c * P, c * P + P)
                    last = product(XB[:, c * P:c * P + P], a_hi[:, j % 3, tok], a_lo[:, j % 3, tok],
                                   wh(WD, j * D, D), wl(WD, j * D, D), j == 0 and c == 0, j == EP - 1, True)
                last.then_inc(down_mm, 1)

            def experts(n, projected):
                pe.wait_ge(h2T_ready, n + 1)
                for j in range(EP + DOWN_LAG):
                    maxima = projected and j < H
                    if j == 1:
                        pe.wait_ge(logits_done, n + 1)
                        if projected:
                            pe.wait_ge(proj_lo, (n + 2) * NPROJ)
                    if j < EP:
                        gate(n, j)
                    if j == 0:
                        pe.wait_ge(combT_ready, n + 1)
                        if projected:
                            pe.wait_ge(proj_lo, (n + 2) * NPROJ - 2)
                    if 1 <= j <= EP:
                        spread_weights(n, j - 1)
                    if maxima:
                        max_scores(n + 1, j, 0)
                    if j < EP:
                        up_product(n, j)
                    if maxima:
                        max_scores(n + 1, j, 1)
                    if j >= DOWN_LAG:
                        experts_down(n, j - DOWN_LAG)
                    if maxima:
                        max_scores(n + 1, j, 2)
                        max_scores(n + 1, j, 3)
                    if projected and j == EP + 1:
                        turn_maxima(n + 1)

            pe.wait_ge(consts_loaded, 80)
            pe.wait_ge(w_lo_done, 7)
            project(0)
            project_units(0, 0, NPROJ)
            pe.wait_ge(proj_lo, NPROJ)
            for h in range(H):
                for c in range(C):
                    max_scores(0, h, c)
            turn_maxima(0)

            def sequence(n, more):
                attend(n)
                route(n, more)
                experts(n, more)

            sequence(0, True)
            with pe.Fori(1, B - 1) as i:
                sequence(i, True)
            sequence(B - 1, False)

        @block.scalar
        def _(act):
            def project(n):
                act.wait_ge(hT_mm, n + 1)
                wait(act, proj_mm, n * NPROJ)
                act.activation(hT[:, :, :].rearrange("p a s -> p (a s)"), half(G0), ACT.Copy).then_inc(hT_ready, 1)
                wait(act, pv_mm, n * H)

            def project_high(n, first, end):
                for k in range(first, end):
                    bank = proj_banks[k % 4]
                    act.wait_ge(proj_mm, n * NPROJ + k + 1)
                    if k < 8:
                        c, side = k // 2, k % 2
                        act.activation(v_hi[:, c, 8 * side:8 * side + 8, 0:E], bank[:, :].rearrange("p (h e) -> p h e", h=8),
                                       ACT.Copy).then_inc(proj_hi, 1)
                    else:
                        pair, w = (k - 8) // 2, k % 2
                        g = pair // 2
                        if pair % 2 == 0 and w == 0:
                            wait(act, placed[g - 2] if g >= 2 else placed[g + 2], 192 * (n + 1) if g >= 2 else 192 * n)
                        act.activation(nat_hi[:, g % 2, w, pair % 2, :], bank[:, :], ACT.Copy).then_inc(proj_hi, 1)

            def copy_maxima(n):
                act.wait_ge(rowmaxT_mm, n + 1)
                wait(act, max_placed, 32 * n)
                wait(act, wgt_mm, n * EP)
                act.activation(rowmaxT[:, :], half(G0)[0:2 * H, 0:S], ACT.Copy).then_inc(rowmaxT_ready, 1)

            def attend(n):
                for step in range(H + TURN + 1):
                    if step < H:
                        for u, (at, cols) in enumerate(((0, 512), (512, 512), (1024, 256))):
                            act.wait_ge(score_mm, n * H * UNITS + step * UNITS + u + 1)
                            if u == 0:
                                used = max(0, step - 2)
                                wait(act, p_lo_dve, n * H + used)
                                wait(act, p_lo_pool, n * H + used)
                            act.activation(p32[:, step % 3, at:at + cols], score_banks[u][:, 0:cols], ACT.Exp,
                                           scale=back[:, SC_SCORE:SC_SCORE + 1]).then_inc(exp_done, 1)
                    h = step - LAG - 1
                    if 0 <= h < H:
                        q, ab = h // 2, h % 2
                        if ab == 0:
                            wait(act, oT_mm, n * PAIRS + max(0, q - 1))
                        act.wait_ge(o32_done, n * H + h + 1)
                        act.activation(o_hl[:, q % 2, 0, :, E * ab:E * ab + E], o32[:, h % 2], ACT.Copy).then_inc(o_hi_done, 1)
                    h = step - TURN
                    if 0 <= h < H and h % 2 == 1:
                        copy_oT(n, h // 2)

            def copy_oT(n, q):
                act.wait_ge(oT_mm, n * PAIRS + q + 1)
                wait(act, y_mm, n * PAIRS + max(0, q - 1))
                act.activation(oT[:, q % 2].rearrange("p a s -> p (a s)"), half(oT_banks[q % 2]), ACT.Copy).then_inc(oT_ready, 1)

            def route(n, more):
                def projections(first, end):
                    if more:
                        project_high(n + 1, first, end)
                if more:
                    project(n + 1)
                projections(0, TURN_AT)
                act.wait_ge(h2T_mm, n + 1)
                wait(act, u_mm, n * EP)
                act.activation(h2T[:, :, :].rearrange("p a s -> p (a s)"), half(S0), ACT.Copy).then_inc(h2T_ready, 1)
                projections(TURN_AT, EXP_AT)
                act.wait_ge(shift_done, n + 1)
                wait(act, exm_done, n)
                act.activation(ex[:, :, :], shifted[:, :, :], ACT.Exp).then_inc(ex_done, 1)
                projections(EXP_AT, SPREAD_AT)
                act.wait_ge(combT_mm, n + 1)
                wait(act, wgt_mm, n * EP)
                act.activation(combT[:, :], half(S2)[:, 0:S], ACT.Copy).then_inc(combT_ready, 1)
                projections(SPREAD_AT, NPROJ)

            def experts(n, more):
                for j in range(EP + 2):
                    if j < EP:
                        act.wait_ge(g_mm, n * EP + j + 1)
                        wait(act, sg_done, n * EP + max(0, j - 1))
                        act.activation(th[:, j % 2, :], gate_banks[j % 2][:, :], ACT.Tanh, scale=back[:, SC_TANH:SC_TANH + 1]).then_inc(th_done, 1)
                        act.wait_ge(u_mm, n * EP + j + 1)
                        wait(act, a32_done, n * EP + max(0, j - 2))
                        act.activation(up[:, j % 3, :], up_banks[j % 2][:, :], ACT.Copy).then_inc(up_done, 1)
                    k = j - 2
                    if k >= 0:
                        act.wait_ge(a32_done, n * EP + k + 1)
                        wait(act, down_mm, n * EP + max(0, k - 2))
                        act.activation(a_hi[:, k % 3, :], a32[:, k % 3, :], ACT.Copy).then_inc(a_hi_done, 1)
                if more:
                    copy_maxima(n + 1)

            act.wait_ge(w_scaling, 8)
            project(0)
            project_high(0, 0, NPROJ)
            copy_maxima(0)

            def sequence(n, more):
                attend(n)
                route(n, more)
                experts(n, more)

            sequence(0, True)
            with act.Fori(1, B - 1) as i:
                sequence(i, True)
            sequence(B - 1, False)

        @block.vector
        def _(dve):
            def norm_stats(n, which, src):
                wait(dve, ln_mv[which], C * n)
                for c in range(C):
                    dve.bn_stats(stats[:, which, c, :], src[:, c, :]).then_inc(ln_stats[which], 1)
                dve.wait_ge(ln_stats[which], C * (n + 1))
                wait(dve, ln_out[which], C * n)
                wait(dve, ln_var[which], n)
                apart(dve)
                for c in range(C):
                    dve.bn_aggr(mv[:, which, c, :], stats[:, which, c, :]).then_inc(ln_mv[which], 1)

            def norm_apply(n, which, src, dst):
                dve.wait_ge(ln_rstd[which], n + 1)
                for c in range(C):
                    dve.tensor_scalar(dst[:, c, :], src[:, c, :], mv[:, which, c, 0:1], rstd[:, which, c:c + 1],
                                      ALU.subtract, ALU.mult).then_inc(ln_out[which], 1)

            def split_norm(n, which, src, hl, hi_sem, lo_sem):
                dve.wait_ge(ln_out[which], C * (n + 1))
                dve.tensor_copy(hl[:, 0], src).then_inc(hi_sem, 1)
                dve.wait_ge(hi_sem, n + 1)
                dve.tensor_tensor(hl[:, 1], src, hl[:, 0], ALU.subtract).then_inc(lo_sem, 1)

            def normalise_input(n):
                dve.wait_ge(x_loaded, 16 * (n + 1))
                norm_stats(n, 0, xt)
                wait(dve, cur_copied, 2 * n)
                norm_apply(n, 0, xt, h32)
                wait(dve, h2T_mm, n - 1)
                split_norm(n, 0, h32[:, :, :], split_hl, h_hi, h_lo)

            def project_low(n, first, end):
                for k in range(first, end):
                    bank = proj_banks[k % 4]
                    dve.wait_ge(proj_hi, n * NPROJ + k + 1)
                    if k < 8:
                        c, side = k // 2, k % 2
                        dve.tensor_tensor(v_lo[:, c, 8 * side:8 * side + 8, :], bank[:, :].rearrange("p (h e) -> p h e", h=8),
                                          v_hi[:, c, 8 * side:8 * side + 8, 0:E], ALU.subtract).then_inc(proj_lo, 1)
                    else:
                        pair, w = (k - 8) // 2, k % 2
                        g = pair // 2
                        if pair % 2 == 0 and w == 0:
                            wait(dve, placed[g - 2] if g >= 2 else placed[g + 2], 192 * (n + 1) if g >= 2 else 192 * n)
                        dve.tensor_tensor(nat_lo[:, g % 2, w, pair % 2, :], bank[:, :], nat_hi[:, g % 2, w, pair % 2, :],
                                          ALU.subtract).then_inc(proj_lo, 1)

            def row_maximum(n, h, c):
                k = h * C + c
                cols, hs = (c + 1) * P, (h % 2) * PAIRS + h // 2
                dve.wait_ge(max_mm, n * H * C + k + 1)
                wait(dve, max_done, n * H * C + max(0, k - 1))
                if k == 0:
                    wait(dve, rowmax_lo, n)
                apart(dve)
                dve.tensor_tensor_reduce(max_junk[:, k % 2, 0:cols], max_banks[k % 2][:, 0:cols], mask[:, S - cols:S],
                                         1.0, NEG, ALU.add, ALU.max, rowmax[:, c, hs:hs + 1]).then_inc(max_done, 1)

            def split_maxima(n):
                dve.wait_ge(max_done, (n + 1) * H * C)
                wait(dve, rowmaxT_mm, n)
                dve.tensor_scalar(rowmax_hl[:, :, 0, :], rowmax[:, :, :], -1.0 / MAX_UNIT, None, ALU.mult).then_inc(rowmax_hi, 1)
                dve.wait_ge(rowmax_hi, n + 1)
                dve.scalar_tensor_tensor(rowmax_hl[:, :, 1, :], rowmax[:, :, :], -1.0 / MAX_UNIT, rowmax_hl[:, :, 0, :],
                                         ALU.mult, ALU.subtract).then_inc(rowmax_lo, 1)

            def attend(n):
                for step in range(H + LAG + 2):
                    h = step - LAG - 2
                    if 0 <= h < H:
                        low(n, h)
                    h = step - LAG - 1
                    if 0 <= h < H:
                        bank = pv_banks[h % 2][:, 0:C * (E + 1)].rearrange("p (c e) -> p c e", c=C)
                        dve.wait_ge(pv_mm, n * H + h + 1)
                        dve.reciprocal(rden[:, h % 2, :].rearrange("p (c a) -> p c a", a=1), bank[:, :, E:E + 1]).then_inc(rden_done, 1)
                        dve.wait_ge(rden_done, n * H + h + 1)
                        wait(dve, o_hi_done, n * H + max(0, h - 1))
                        wait(dve, o_lo_done, n * H + max(0, h - 1))
                        dve.tensor_tensor(o32[:, h % 2], bank[:, :, 0:E],
                                          rden[:, h % 2, :].rearrange("p (c a) -> p c a", a=1).to_broadcast([P, C, E]), ALU.mult).then_inc(o32_done, 1)
                    h = step - 1
                    if 0 <= h < H:
                        dve.wait_ge(masked, n * H + h + 1)
                        wait(dve, pv_mm, n * H + max(0, h - 2))
                        dve.tensor_copy(p_hi[:, h % 3, :], p32[:, h % 3, :]).then_inc(p_hi_done, 1)
                        dve.wait_ge(p_hi_done, n * H + h + 1)
                        dve.tensor_tensor(p_lo[:, h % 3, 0:S], p32[:, h % 3, 0:S], p_hi[:, h % 3, 0:S], ALU.subtract).then_inc(p_lo_dve, 1)

            def low(n, h):
                q, ab = h // 2, h % 2
                cols = slice(E * ab, E * ab + E)
                dve.wait_ge(o_hi_done, n * H + h + 1)
                wait(dve, oT_mm, n * PAIRS + max(0, q - 1))
                dve.tensor_tensor(o_hl[:, q % 2, 1, :, cols], o32[:, h % 2], o_hl[:, q % 2, 0, :, cols], ALU.subtract).then_inc(o_lo_done, 1)

            def residual(n, more):
                dve.wait_ge(y_mm, PAIRS * (n + 1))
                dve.wait_ge(cur_copied, 2 * n + 2)
                wait(dve, out_stored, 16 * n)
                dve.scalar_tensor_tensor(y0[:, :, :], XB[:, :].rearrange("p (c d) -> p c d", c=C), back[:, SC_Y:SC_Y + 1],
                                         h_cur[:, :, :], ALU.mult, ALU.add).then_inc(y0_done, 1)
                dve.wait_ge(y0_done, n + 1)
                norm_stats(n, 1, y0)
                if more:
                    project_low(n + 1, 0, NORM_AT[0])
                wait(dve, yg_done, n)
                norm_apply(n, 1, y0, y0)
                dve.wait_ge(ln_out[1], C * (n + 1))
                wait(dve, x1_done, n)
                dve.tensor_tensor(y0[:, :, :], y0[:, :, :], gam[:, :, :].to_broadcast([P, C, D]), ALU.mult).then_inc(yg_done, 1)
                dve.wait_ge(yg_done, n + 1)
                wait(dve, out_ready, n)
                dve.tensor_tensor(x1[:, :, :], y0[:, :, :], xb_cur[:, :, :], ALU.add).then_inc(x1_done, 1)
                dve.wait_ge(x1_done, n + 1)
                norm_stats(n, 2, x1)
                if more:
                    project_low(n + 1, NORM_AT[0], NORM_AT[1])
                wait(dve, h2_lo, n)
                dve.wait_ge(x1_done, n + 1)
                norm_apply(n, 2, x1, y0)
                dve.wait_ge(hT_mm, n + 2 if more else n + 1)
                split_norm(n, 2, y0[:, :, :], split_hl, h2_hi, h2_lo)

            def route(n, more):
                if more:
                    project_low(n + 1, NORM_AT[1], CHOOSE_AT)
                dve.wait_ge(logit_mm, n + 1)
                wait(dve, shift_done, n)
                wait(dve, chosen_done, n)
                dve.tensor_scalar(logits[:, :, :], S1[:, 0:C * NE].rearrange("p (c e) -> p c e", c=C), w_back[:, WG:WG + 1], None,
                                  ALU.mult).then_inc(logits_done, 1)
                dve.wait_ge(logits_done, n + 1)
                wait(dve, drop_done, C * n)
                apart(dve)
                for c in range(C):
                    dve.max(top8[:, c, :], logits[:, c, :]).then_inc(top_done, 1)
                dve.wait_ge(top_done, C * (n + 1))
                apart(dve)
                for c in range(C):
                    dve.match_replace(dropped[:, c, :], top8[:, c, :], logits[:, c, :], NEG).then_inc(drop_done, 1)
                wait(dve, ex_done, n)
                dve.tensor_tensor(shifted[:, :, :], logits[:, :, :], top8[:, :, 0:1].to_broadcast([P, C, NE]), ALU.subtract).then_inc(shift_done, 1)
                dve.wait_ge(drop_done, C * (n + 1))
                wait(dve, exm_done, n)
                dve.tensor_tensor(chosen[:, :, :], dropped[:, :, :], logits[:, :, :], ALU.not_equal).then_inc(chosen_done, 1)
                if more:
                    project_low(n + 1, CHOOSE_AT, WEIGH_AT)
                dve.wait_ge(chosen_done, n + 1)
                dve.wait_ge(ex_done, n + 1)
                wait(dve, comb_done, n)
                dve.tensor_tensor(exm[:, :, :], ex[:, :, :], chosen[:, :, :], ALU.mult).then_inc(exm_done, 1)
                dve.wait_ge(exm_done, n + 1)
                wait(dve, exinv_done, n)
                dve.tensor_reduce(exsum[:, :], exm[:, :, :], AX.X, ALU.add).then_inc(exsum_done, 1)
                dve.wait_ge(exsum_done, n + 1)
                dve.reciprocal(exinv[:, :], exsum[:, :]).then_inc(exinv_done, 1)
                dve.wait_ge(exinv_done, n + 1)
                wait(dve, comb_split, 5 * n)
                wait(dve, combT_mm, n)
                dve.tensor_tensor(comb[:, :, :], exm[:, :, :], exinv[:, :].rearrange("p (c a) -> p c a", a=1).to_broadcast([P, C, NE]),
                                  ALU.mult).then_inc(comb_done, 1)
                dve.wait_ge(comb_done, n + 1)
                dve.tensor_copy(comb_parts[:, :, 0, :], comb[:, :, :]).then_inc(comb_split, 1)
                dve.wait_ge(comb_split, 5 * n + 1)
                dve.tensor_tensor(comb_rest[:, :, :], comb[:, :, :], comb_parts[:, :, 0, :], ALU.subtract).then_inc(comb_split, 1)
                dve.wait_ge(comb_split, 5 * n + 2)
                dve.tensor_copy(comb_parts[:, :, 1, :], comb_rest[:, :, :]).then_inc(comb_split, 1)
                dve.wait_ge(comb_split, 5 * n + 3)
                dve.tensor_tensor(comb_parts[:, :, 2, :], comb_rest[:, :, :], comb_parts[:, :, 1, :], ALU.subtract).then_inc(comb_split, 2)
                if more:
                    project_low(n + 1, WEIGH_AT, NPROJ)

            def experts(n, more):
                for j in range(EP + 1):
                    maxima = more and j < H
                    if more and j == EP:
                        split_maxima(n + 1)
                    if j < EP:
                        dve.wait_ge(th_done, n * EP + j + 1)
                        wait(dve, su_done, n * EP + max(0, j - 1))
                        dve.scalar_tensor_tensor(sg[:, j % 2, :], th[:, j % 2, :], 1.0, gate_banks[j % 2][:, :], ALU.add, ALU.mult).then_inc(sg_done, 1)
                    if maxima:
                        row_maximum(n + 1, j, 0)
                        row_maximum(n + 1, j, 1)
                    k = j - 1
                    if k >= 0:
                        dve.wait_ge(su_done, n * EP + k + 1)
                        dve.wait_ge(wgt_mm, n * EP + k + 1)
                        wait(dve, a_hi_done, n * EP + max(0, k - 2))
                        wait(dve, a_lo_done, n * EP + max(0, k - 2))
                        dve.tensor_tensor(a32[:, k % 3, :], weight_bank[:, :], up[:, k % 3, :], ALU.mult).then_inc(a32_done, 1)
                    if maxima:
                        row_maximum(n + 1, j, 2)
                        row_maximum(n + 1, j, 3)
                dve.wait_ge(down_mm, EP * (n + 1))
                dve.wait_ge(h2_lo, n + 1)
                dve.scalar_tensor_tensor(y0[:, :, :], XB[:, :].rearrange("p (c d) -> p c d", c=C), back[:, SC_OUT:SC_OUT + 1],
                                         x1[:, :, :], ALU.mult, ALU.add).then_inc(out_ready, 1)

            dve.memset(w_absmax[:, :], 1.0).then_inc(consts_set, 1)
            dve.wait_ge(consts_set, 1)
            for w in range(7):
                dve.wait_ge(w_loaded, 16 * 7)
                dve.tensor_reduce(w_absmax[:, w:w + 1], raw[:, WAT[w]:WAT[w] + WCOLS[w]], AX.X, ALU.max,
                                  apply_absolute_value=True).then_inc(w_maxed, 1)
            dve.wait_ge(w_allmaxed, 1)
            dve.tensor_scalar(w_allmax[:, :], w_allmax[:, :], 2.0 ** -100, None, ALU.max).then_inc(w_scaling, 1)
            dve.wait_ge(w_scaling, 1)
            dve.tensor_scalar(w_pow[:, :].bitcast(I32), w_allmax[:, :].bitcast(I32), 0x7F800000, None, ALU.bitwise_and).then_inc(w_scaling, 1)
            dve.wait_ge(w_scaling, 2)
            dve.tensor_scalar(w_back[:, :], w_pow[:, :], 0.125, None, ALU.mult).then_inc(w_scaling, 1)
            dve.wait_ge(w_scaling, 3)
            dve.reciprocal(w_scale[:, :], w_back[:, :]).then_inc(w_scaling, 1)

            def pair_product(dst, a, b, factor):
                return dve.scalar_tensor_tensor(back[:, dst:dst + 1], a, factor, b, ALU.mult, ALU.mult)

            def wb(w):
                return w_back[:, w:w + 1]
            pair_product(SC_SCORE, wb(WQ), wb(WK), float(E) ** -0.5).then_inc(w_scaling, 1)
            pair_product(SC_Y, wb(WV), wb(WO), 1.0).then_inc(w_scaling, 1)
            pair_product(SC_GU2, wb(WGU), wb(WGU), 0.5 / COMB_SHIFT).then_inc(w_scaling, 1)
            dve.tensor_scalar(back[:, SC_TANH:SC_TANH + 1], wb(WGU), 0.5, None, ALU.mult).then_inc(w_scaling, 1)
            dve.wait_ge(w_scaling, 8)
            pair_product(SC_OUT, back[:, SC_GU2:SC_GU2 + 1], wb(WD), 1.0).then_inc(w_scaling, 1)
            for w in range(7):
                src = raw[:, WAT[w]:WAT[w] + WCOLS[w]]
                scale = w_scale[:, w:w + 1]
                dve.tensor_scalar(wh(w, 0, WCOLS[w]), src, scale, None, ALU.mult).then_inc(w_hi_done, 1)
                dve.wait_ge(w_hi_done, w + 1)
                dve.scalar_tensor_tensor(wl(w, 0, WCOLS[w]), src, scale, wh(w, 0, WCOLS[w]), ALU.mult, ALU.subtract).then_inc(w_lo_done, 1)
            dve.wait_ge(w_lo_done, 7)
            dve.memset(KB[E:P].rearrange("p a b s -> p (a b s)").bitcast(F32), 0.0).then_inc(consts_set, 1)
            dve.memset(QB[E:P].rearrange("p a b s -> p (a b s)").bitcast(F32), 0.0).then_inc(consts_set, 1)
            dve.wait_ge(consts_set, 3)
            dve.memset(KB[E:E + 2].rearrange("p a b s -> p (a b s)"), MAX_UNIT).then_inc(consts_set, 1)
            dve.memset(v_hi[:, :, :, E:E + 1], 1.0).then_inc(consts_set, 1)
            dve.memset(comb_parts[:, :, 3, :], 0.0).then_inc(consts_set, 1)
            dve.wait_ge(consts_set, 6)
            dve.wait_ge(consts_loaded, 80)

            normalise_input(0)
            project_low(0, 0, NPROJ)
            for h in range(H):
                for c in range(C):
                    row_maximum(0, h, c)
            split_maxima(0)

            def sequence(n, more):
                if more:
                    normalise_input(n + 1)
                attend(n)
                residual(n, more)
                route(n, more)
                experts(n, more)

            sequence(0, True)
            with dve.Fori(1, B - 1) as i:
                sequence(i, True)
            sequence(B - 1, False)

        @block.gpsimd
        def _(pool):
            def inverse_deviation(n, which, eps):
                pool.wait_ge(ln_mv[which], C * (n + 1))
                apart(pool)
                pool.tensor_scalar(var_eps[:, which, :].rearrange("p (c a) -> p c a", a=1), mv[:, which, :, 1:2], eps, 0.0, ALU.add, ALU.add).then_inc(ln_var[which], 1)
                pool.wait_ge(ln_var[which], n + 1)
                wait(pool, ln_out[which], C * n)
                pool.tensor_tensor(rstd[:, which, :], var_eps[:, which, :], minus_half[:, :], ALU.pow).then_inc(ln_rstd[which], 1)

            def normalise_input(n):
                inverse_deviation(n, 0, LN_EPS)

            def keep_current(n):
                pool.wait_ge(h_lo, n + 1)
                wait(pool, x1_done, n)
                apart(pool)
                pool.tensor_copy(h_cur[:, :, :], h32[:, :, :]).then_inc(cur_copied, 1)
                pool.wait_ge(x_loaded, 16 * (n + 1))
                pool.tensor_tensor(xb_cur[:, :, :], xt[:, :, :], bet[:, :, :].to_broadcast([P, C, D]), ALU.add).then_inc(cur_copied, 1)

            def attend(n):
                for step in range(H + 1):
                    if step < H:
                        pool.wait_ge(exp_done, n * H * UNITS + UNITS * (step + 1))
                        apart(pool)
                        p = p32[:, step % 3, :]
                        keep = dict(compare_op=ALU.is_ge, fill=0.0, base=0, channel_multiplier=-1)
                        far = p[:, 0:1024].rearrange("p (a s) -> p a s", a=2)[:, :, 0:P]
                        pool.affine_select(far, far, pattern=[[0, 2], [1, P]], **keep).then_inc(diag_pair, 1)
                        near = p[:, 896:1152].rearrange("p (a s) -> p a s", a=2)
                        pool.affine_select(near, near, pattern=[[0, 2], [1, P]], **keep).then_inc(masked, 1)
                    h = step - 1
                    if h >= 0:
                        pool.wait_ge(p_hi_done, n * H + h + 1)
                        wait(pool, pv_mm, n * H + max(0, h - 2))
                        pool.tensor_tensor(p_lo[:, h % 3, S:PCOLS], p32[:, h % 3, S:PCOLS], p_hi[:, h % 3, S:PCOLS], ALU.subtract).then_inc(p_lo_pool, 1)

            def experts(n):
                for j in range(EP + 2):
                    if j < EP:
                        pool.wait_ge(up_done, n * EP + j + 1)
                        pool.wait_ge(sg_done, n * EP + j + 1)
                        pool.tensor_tensor(up[:, j % 3, :], sg[:, j % 2, :], up[:, j % 3, :], ALU.mult).then_inc(su_done, 1)
                    k = j - 2
                    if k >= 0:
                        pool.wait_ge(a_hi_done, n * EP + k + 1)
                        wait(pool, down_mm, n * EP + max(0, k - 2))
                        pool.tensor_tensor(a_lo[:, k % 3, :], a32[:, k % 3, :], a_hi[:, k % 3, :], ALU.subtract).then_inc(a_lo_done, 1)

            pool.memset(minus_half[:, :], -0.5).then_inc(pool_set, 1)
            pool.wait_ge(w_maxed, 7)
            pool.partition_all_reduce(w_allmax[:, :], w_absmax[:, :], P, bass.bass_isa.ReduceOp.absmax).then_inc(w_allmaxed, 1)
            pool.wait_ge(pool_set, 1)
            pool.wait_ge(consts_loaded, 80)
            normalise_input(0)

            def sequence(n, more):
                keep_current(n)
                if more:
                    normalise_input(n + 1)
                attend(n)
                inverse_deviation(n, 1, ATTN_LN_EPS)
                inverse_deviation(n, 2, LN_EPS)
                experts(n)

            sequence(0, True)
            with pool.Fori(1, B - 1) as i:
                sequence(i, True)
            sequence(B - 1, False)


_INS = ("L0_attn_x", "L0_attn_Wq", "L0_attn_Wk", "L0_attn_Wv", "L0_attn_Wo", "L0_attn_gamma", "L0_attn_beta",
        "L0_ffn_gate_w", "L0_ffn_gate_up_w", "L0_ffn_down_w")


def kernel(**inputs):
    import concourse.bacc as bacc
    from concourse.bass_utils import run_bass_kernel_spmd

    x, wq, wk, wv, wo, gamma, beta, gate_w, gate_up_w, down_w = (np.asarray(inputs[n]) for n in _INS)
    cont = np.ascontiguousarray

    def by_width(w):
        return cont(w.transpose(1, 0, 2).reshape(D, H * E))
    gu = gate_up_w.reshape(EP, 2, 2, ED, D).transpose(4, 0, 2, 1, 3)
    select = np.zeros((P, EP, P), np.float16)
    for part in range(3):
        for e in range(NE):
            select[part * NE + e, e // 2, (e % 2) * ED:(e % 2) * ED + ED] = COMB_SHIFT
    col = np.arange(S) - (S - P)
    arrays = {
        "x": cont(x), "wq": by_width(wq), "wk": by_width(wk), "wv": by_width(wv),
        "wo": cont(wo.reshape(PAIRS, P, D).transpose(1, 0, 2).reshape(P, PAIRS * D)),
        "gamma": cont(np.broadcast_to(gamma, (P, 1, D))), "beta": cont(np.broadcast_to(beta, (P, 1, D))),
        "gate": cont(gate_w.T), "gate_up": cont(gu.reshape(D, EP * 4 * ED)),
        "down": cont(down_w.reshape(EP, 2, D, ED).transpose(1, 3, 0, 2).reshape(P, EP * D)),
        "ident": np.eye(P, dtype=np.float16),
        "mask": np.where(col[None, :] > np.arange(P)[:, None], np.float32(NEG), np.float32(0.0)),
        "select": select,
    }
    nc = bacc.Bacc("TRN2", target_bir_lowering=False, num_devices=1)
    args = [nc.dram_tensor(f"in_{n}", a.shape, mybir.dt.from_np(a.dtype), kind="ExternalInput").ap() for n, a in arrays.items()]
    out = nc.dram_tensor("out_y", (B, S, D), F32, kind="ExternalOutput").ap()
    layer(nc, *args, out)
    r = run_bass_kernel_spmd(nc, [{f"in_{n}": a for n, a in arrays.items()}], core_ids=[0])
    return r.results[0]["out_y"]
```

```python
from contextlib import ExitStack

import numpy as np
import concourse.bass as bass
from concourse import mybir

F32, F16, I32 = mybir.dt.float32, mybir.dt.float16, mybir.dt.int32
ALU = mybir.AluOpType
ACT = mybir.ActivationFunctionType
AX = mybir.AxisListType

P = 128
B, S, D = 16, 512, 128
H, E = 16, 64
PAIRS = H // 2
C = S // P
NE, TOPK, ED = 32, 8, 64
EP = NE // 2
GROUPS = 4
LN_EPS, ATTN_LN_EPS = 1e-5, 1e-3
MAX_UNIT = 2.0 ** 13
COMB_SHIFT = 2.0 ** -8
NEG = -3.0e38
NORMALISE_AT = 5
LAG = 3
TURN = 6
DOWN_LAG = 3
MAX_CHUNKS = ((3,), (0, 2), (1,))
MAX_UNITS = len(MAX_CHUNKS)
MAX_STEP = 4
MAX_END = -(-H * MAX_UNITS // MAX_STEP)
UNITS = 3
PCOLS = 1280
NKQ = 2 * PAIRS
NPROJ = NKQ + 8
TAIL_AT = (2, 4, 6)
TURN_AT = 10
LOGITS_AT = 14
EXP_AT = 14
SPREAD_AT = 20
NORM_AT = (8, 10)
CHOOSE_AT = 12
WEIGH_AT = 16


def tail_from(s):
    return TAIL_AT[s - 1] if s else 0


def maxima_of(j):
    return [divmod(k, MAX_UNITS) for k in range(MAX_STEP * j, min(MAX_STEP * (j + 1), H * MAX_UNITS))]


def max_col(c):
    return P if c == 2 else 0


def prob_col(t, c):
    return {0: c * P, 1: 512 + (c - 1) * P, 2: 1024 + (c - 2) * P, 3: 896}[t]


def layer(nc, x, wq, wk, wv, wo, gamma, beta, gate, gate_up, down, ident_c, mask_c, select_c, out):
    with ExitStack() as ctx:
        def sb(name, shape, dt):
            return ctx.enter_context(nc.sbuf_tensor(name, shape, dt))

        def sem(name):
            return ctx.enter_context(nc.semaphore(name))

        ident = sb("ident", [P, P], F16)
        mask = sb("mask", [P, S], F32)
        select = sb("select", [P, EP, P], F16)
        score_ops = sb("score_ops", [P, 4, 2, PAIRS, S], F16)
        KA, KB, QA, QB = (score_ops[:, n] for n in range(4))
        raw = score_ops[:, :, :, :, :].rearrange("p a b c d -> p (a b c d)").bitcast(F32)
        WCOLS = [D * 8, D * 8, D * 8, D * 8, EP * 2 * P, EP * D, NE]
        WQ, WK, WV, WO, WGU, WD, WG = range(7)
        WAT = [sum(WCOLS[:n]) for n in range(7)]
        w_hi = sb("w_hi", [P, sum(WCOLS)], F16)
        w_lo = sb("w_lo", [P, sum(WCOLS)], F16)
        w_absmax = sb("w_absmax", [P, 8], F32)
        w_allmax = sb("w_allmax", [P, 8], F32)
        w_pow = sb("w_pow", [P, 8], F32)
        w_scale = sb("w_scale", [P, 8], F32)
        w_back = sb("w_back", [P, 8], F32)
        back = sb("back", [P, 8], F32)
        SC_SCORE, SC_Y, SC_OUT = range(3)
        gam = sb("gam", [P, 1, D], F32)
        bet = sb("bet", [P, 1, D], F32)
        minus_half = sb("minus_half", [P, C], F32)

        xt = sb("xt", [P, C, D], F32)
        h32 = sb("h32", [P, C, D], F32)
        h_cur = sb("h_cur", [P, C, D], F32)
        xb_cur = sb("xb_cur", [P, C, D], F32)
        split_hl = sb("split_hl", [P, 2, C, D], F16)
        hT = sb("hT", [P, 2, S], F16)
        stats = sb("stats", [P, 3, C, 6], F32)
        mv = sb("mv", [P, 3, C, 2], F32)
        var_eps = sb("var_eps", [P, 3, C], F32)
        rstd = sb("rstd", [P, 3, C], F32)
        nat_hi = sb("nat_hi", [P, 2, 2, 2, S], F16)
        nat_lo = sb("nat_lo", [P, 2, 2, 2, S], F16)
        v_hi = sb("v_hi", [P, C, H, E + 1], F16)
        v_lo = sb("v_lo", [P, C, H, E], F16)
        max_junk = sb("max_junk", [P, 2, S], F16)
        rowmax = sb("rowmax", [P, C, H], F32)
        rowmax_hl = sb("rowmax_hl", [P, C, 2, H], F16)
        room = sb("room", [P, 6 * PCOLS], F32)

        def carve(at, slots, cols, dt):
            words = slots * cols // (1 if dt is F32 else 2)
            return room[:, at:at + words].bitcast(dt).rearrange("p (a b) -> p a b", a=slots)
        p32 = carve(0, 3, PCOLS, F32)
        p_hi, p_lo = (carve(at, 3, PCOLS, F16) for at in (3 * PCOLS, 3 * PCOLS + 3 * PCOLS // 2))
        sg = carve(0, 2, S, F32)
        rowmaxT = carve(2 * S, 1, S, F16)[0:2 * H, 0, :]
        up, a32 = (carve(4 * S + 3 * S * n, 3, S, F32) for n in range(2))
        a_hi, a_lo = (carve(10 * S + n * 3 * S // 2, 3, S, F16) for n in range(2))
        logits, dropped, chosen, shifted, ex, exm, comb, comb_rest = (
            carve(13 * S + n * C * NE, C, NE, F32) for n in range(8))
        rden = sb("rden", [P, 2, C], F32)
        o32 = sb("o32", [P, 2, C, E], F32)
        o_hl = sb("o_hl", [P, 2, 2, C, 2 * E], F16)
        oT = sb("oT", [P, 2, 2, S], F16)
        y0 = sb("y0", [P, C, D], F32)
        x1 = sb("x1", [P, C, D], F32)
        h2T = sb("h2T", [P, 2, S], F16)
        top8 = sb("top8", [P, C, TOPK], F32)
        exsum = sb("exsum", [P, C], F32)
        exinv = sb("exinv", [P, C], F32)
        comb_parts = sb("comb_parts", [P, C, 4, NE], F16)
        combT = sb("combT", [P, S], F16)

        S0, S1, S2, P0, P1, G0, G1, XB = (
            ctx.enter_context(nc.psum_tensor(f"bank_{n}", [P, S], F32)) for n in ("s0", "s1", "s2", "p0", "p1", "g0", "g1", "x"))
        score_banks = [S0, S1, S2]
        pv_banks = [P0, P1]
        proj_banks, input_bank = [S0, S1, S2, P0], S2
        expert_bank, logit_bank, comb_bank = G0, G1, G0
        oT_banks = [G0, G1]
        gate_banks, up_banks, weight_bank = [S0, S1], [S2, P0], P1
        max_banks = [G0, G1]

        def half(bank):
            return bank[:, :].bitcast(F16)

        waits_met = sem("waits_met")
        consts_loaded = sem("consts_loaded")
        w_loaded = [sem(f"w_loaded{w}") for w in range(7)]
        w_maxed = sem("w_maxed")
        w_allmaxed = sem("w_allmaxed")
        w_scaling = sem("w_scaling")
        w_hi_done = sem("w_hi_done")
        w_lo_done = sem("w_lo_done")
        consts_set = sem("consts_set")
        absmax_set, zeros_set = sem("absmax_set"), sem("zeros_set")
        pool_set = sem("pool_set")
        x_loaded, cur_copied = sem("x_loaded"), sem("cur_copied")
        diag_pair = sem("diag_pair")
        ln_stats = [sem(f"ln{n}_stats") for n in range(3)]
        ln_mv = [sem(f"ln{n}_mv") for n in range(3)]
        ln_var = [sem(f"ln{n}_var") for n in range(3)]
        ln_rstd = [sem(f"ln{n}_rstd") for n in range(3)]
        ln_out = [sem(f"ln{n}_out") for n in range(3)]
        h_hi, h_lo = sem("h_hi"), sem("h_lo")
        hT_mm, hT_ready = sem("hT_mm"), sem("hT_ready")
        proj_mm, proj_hi, proj_lo = sem("proj_mm"), sem("proj_hi"), sem("proj_lo")
        placed = [sem(f"placed{g}") for g in range(GROUPS)]
        max_mm, max_done = sem("max_mm"), sem("max_done")
        rowmax_hi, rowmax_lo = sem("rowmax_hi"), sem("rowmax_lo")
        rowmaxT_mm, rowmaxT_ready, max_placed = sem("rowmaxT_mm"), sem("rowmaxT_ready"), sem("max_placed")
        score_mm, exp_done, masked = sem("score_mm"), sem("exp_done"), sem("masked")
        p_hi_done, p_lo_dve, p_lo_pool = sem("p_hi_done"), sem("p_lo_dve"), sem("p_lo_pool")
        pv_mm, rden_done, o32_done = sem("pv_mm"), sem("rden_done"), sem("o32_done")
        o_hi_done, o_lo_done = sem("o_hi_done"), sem("o_lo_done")
        oT_mm, oT_ready, y_mm = sem("oT_mm"), sem("oT_ready"), sem("y_mm")
        y0_done, yg_done, x1_done = sem("y0_done"), sem("yg_done"), sem("x1_done")
        h2_hi, h2_lo, h2T_mm, h2T_ready = sem("h2_hi"), sem("h2_lo"), sem("h2T_mm"), sem("h2T_ready")
        logit_mm, logits_done, top_done = sem("logit_mm"), sem("logits_done"), sem("top_done")
        drop_done, chosen_done, shift_done = sem("drop_done"), sem("chosen_done"), sem("shift_done")
        ex_done, exm_done, exsum_done, exinv_done = sem("ex_done"), sem("exm_done"), sem("exsum_done"), sem("exinv_done")
        comb_done, comb_split = sem("comb_done"), sem("comb_split")
        combT_mm, combT_ready = sem("combT_mm"), sem("combT_ready")
        g_mm, u_mm, wgt_mm = sem("g_mm"), sem("u_mm"), sem("wgt_mm")
        up_done, sg_done, su_done = sem("up_done"), sem("sg_done"), sem("su_done")
        a32_done, a_hi_done, a_lo_done, down_mm = sem("a32_done"), sem("a_hi_done"), sem("a_lo_done"), sem("down_mm")
        out_ready, out_stored = sem("out_ready"), sem("out_stored")

        def wh(w, a, n):
            return w_hi[:, WAT[w] + a:WAT[w] + a + n]

        def wl(w, a, n):
            return w_lo[:, WAT[w] + a:WAT[w] + a + n]

        def wait(eng, s, value):
            if not (isinstance(value, int) and value <= 0):
                eng.wait_ge(s, value)

        def apart(eng):
            eng.sem_inc(waits_met, 1)

        block = ctx.enter_context(nc.Block())

        @block.sync
        def _(sp):
            sp.dma_start(xt[:, :, :], x[0:1].rearrange("a (c p) d -> p (a c) d", p=P)).then_inc(x_loaded, 16)
            for w, src in enumerate((wq, wk, wv, wo, gate_up, down, gate)):
                sp.dma_start(raw[:, WAT[w]:WAT[w] + WCOLS[w]], src).then_inc(w_loaded[w], 16)
            sp.dma_start(ident[:, :], ident_c).then_inc(consts_loaded, 16)
            sp.dma_start(mask[:, :], mask_c).then_inc(consts_loaded, 16)
            sp.dma_start(select[:, :, :], select_c).then_inc(consts_loaded, 16)
            sp.dma_start(gam[:, :, :], gamma).then_inc(consts_loaded, 16)
            sp.dma_start(bet[:, :, :], beta).then_inc(consts_loaded, 16)

            def load_x(n):
                wait(sp, ln_out[0], C * n)
                apart(sp)
                wait(sp, cur_copied, 2 * n)
                apart(sp)
                sp.dma_start(xt[:, :, :], x[bass.ds(n, 1)].rearrange("a (c p) d -> p (a c) d", p=P)).then_inc(x_loaded, 16)

            def place_qk(n):
                wait(sp, score_mm, n * UNITS * H)
                sp.wait_ge(w_lo_done, 7)
                sp.wait_ge(consts_set, 4)
                for g in range(GROUPS):
                    done = n * NPROJ + 4 * (g + 1)
                    sp.wait_ge(proj_hi, done)
                    sp.wait_ge(proj_lo, done)
                    for ab in range(2):
                        rows = slice(E * ab, E * ab + E)
                        to = slice(2 * g, 2 * g + 2)
                        k_h, q_h = nat_hi[rows, g % 2, 0], nat_hi[rows, g % 2, 1]
                        k_l, q_l = nat_lo[rows, g % 2, 0], nat_lo[rows, g % 2, 1]
                        for dst, lower, src in ((KA, 0, k_h), (KA, 1, k_l), (KB, 0, k_h), (QA, 0, q_h), (QA, 1, q_h), (QB, 0, q_l)):
                            sp.dma_start(dst[E * lower:E * lower + E, ab, to, :], src).then_inc(placed[g], 16)

            def place_max(n):
                sp.wait_ge(rowmaxT_ready, n + 1)
                for part in range(2):
                    sp.dma_start(QB[E + part:E + part + 1].rearrange("a b p s -> a (b p) s"),
                                 rowmaxT[H * part:H * part + H, :]).then_inc(max_placed, 16)

            def store(n):
                sp.wait_ge(out_ready, n + 1)
                apart(sp)
                sp.dma_start(out[bass.ds(n, 1)].rearrange("a (c p) d -> p (a c) d", p=P), y0[:, :, :]).then_inc(out_stored, 16)

            place_qk(0)
            load_x(1)
            place_max(0)
            with sp.Fori(1, B - 1) as i:
                place_qk(i)
                load_x(i + 1)
                place_max(i)
                store(i - 1)
            place_qk(B - 1)
            place_max(B - 1)
            store(B - 2)
            store(B - 1)
            sp.wait_ge(out_stored, 16 * B)

        @block.tensor
        def _(pe):
            def mm(dst, lhsT, rhs, start, stop, shared=False):
                return pe.matmul(dst, lhsT, rhs, start=start, stop=stop, skip_group_check=shared)

            def product(dst, l_hi, l_lo, r_hi, r_lo, start=True, stop=True, shared=False):
                mm(dst, l_hi, r_hi, start, False, shared)
                mm(dst, l_hi, r_lo, False, False, shared)
                return mm(dst, l_lo, r_hi, False, stop, shared)

            def transpose_split(dst, hi_lo):
                for part in range(2):
                    for c in range(C):
                        last = pe.transpose(half(dst)[:, part * S + c * P:part * S + c * P + P], hi_lo[:, part, c, :], ident[:, :])
                return last

            def project(n):
                wait(pe, exp_done, n * H * UNITS)
                pe.wait_ge(h_lo, n + 1)
                transpose_split(input_bank, split_hl).then_inc(hT_mm, 1)

            def project_units(n, first, end):
                for k in range(first, end):
                    bank = proj_banks[k % 4]
                    if k == 0:
                        pe.wait_ge(hT_ready, n + 1)
                    if k == 3:
                        wait(pe, o32_done, n * H - 1)
                    if k >= 4:
                        pe.wait_ge(proj_lo, n * NPROJ + k - 3)
                    if k >= NKQ:
                        c, side = (k - NKQ) // 2, k % 2
                        hc = slice(c * P, c * P + P)
                        last = product(bank[:, :], hT[:, 0, hc], hT[:, 1, hc], wh(WV, side * S, S), wl(WV, side * S, S))
                    else:
                        pair, w = k // 2, (WK, WQ)[k % 2]
                        last = product(bank[:, :], wh(w, pair * P, P), wl(w, pair * P, P), hT[:, 0, :], hT[:, 1, :])
                    last.then_inc(proj_mm, 1)

            def max_scores(n, h, u):
                k, pair, ab = h * MAX_UNITS + u, h // 2, h % 2
                if h % 4 == 0 and u == 0:
                    pe.wait_ge(placed[h // 4], 192 * (n + 1))
                if k >= 2:
                    pe.wait_ge(max_done, n * H * MAX_UNITS + k - 1)
                for c in MAX_CHUNKS[u]:
                    cols, at = (c + 1) * P, max_col(c)
                    last = mm(max_banks[k % 2][:, at:at + cols], QA[:, ab, pair, c * P:c * P + P], KA[:, ab, pair, 0:cols], True, True)
                last.then_inc(max_mm, 1)

            def turn_maxima(n):
                pe.wait_ge(rowmax_lo, n + 1)
                for c in range(C):
                    last = pe.transpose(half(G0)[0:2 * H, c * P:c * P + P],
                                        rowmax_hl[:, c].rearrange("p a h -> p (a h)"), ident[:, :])
                last.then_inc(rowmaxT_mm, 1)

            def scores(n, h):
                pair, ab = h // 2, h % 2
                for u, chunks in enumerate(((0,), (1, 3), (2,))):
                    k = h * UNITS + u
                    if k >= UNITS:
                        pe.wait_ge(exp_done, n * H * UNITS + k - 2)
                    for t in chunks:
                        cols, at = S - t * P, (384 if t == 3 else 0)
                        dst = score_banks[u][:, at:at + cols]
                        keys = slice(t * P, t * P + P)
                        mm(dst, KA[:, ab, pair, keys], QA[:, ab, pair, t * P:S], True, False)
                        last = mm(dst, KB[:, ab, pair, keys], QB[:, ab, pair, t * P:S], False, True)
                    last.then_inc(score_mm, 1)

            def times_v(n, h):
                if h >= 2:
                    pe.wait_ge(o32_done, n * H + h - 1)
                pe.wait_ge(p_lo_dve, n * H + h + 1)
                pe.wait_ge(p_lo_pool, n * H + h + 1)
                if h == 1:
                    wait(pe, a32_done, n * EP)
                bank = pv_banks[h % 2]
                for c in range(C):
                    dst = bank[:, c * (E + 1):(c + 1) * (E + 1)]
                    for t in range(c + 1):
                        at = prob_col(t, c)
                        ph, pl = p_hi[:, h % 3, at:at + P], p_lo[:, h % 3, at:at + P]
                        mm(dst, ph, v_hi[:, t, h, :], t == 0, False)
                        mm(dst[:, 0:E], ph, v_lo[:, t, h, :], False, False)
                        last = mm(dst, pl, v_hi[:, t, h, :], False, t == c)
                last.then_inc(pv_mm, 1)

            def turn_heads(n, q):
                if q >= 2:
                    pe.wait_ge(oT_ready, n * PAIRS + q - 1)
                pe.wait_ge(o_lo_done, n * H + 2 * q + 2)
                pe.wait_ge(o_hi_done, n * H + 2 * q + 2)
                transpose_split(oT_banks[q % 2], o_hl[:, q % 2]).then_inc(oT_mm, 1)

            def times_wo(n, q):
                pe.wait_ge(oT_ready, n * PAIRS + q + 1)
                if q == 0:
                    wait(pe, out_ready, n)
                for c in range(C):
                    tok = slice(c * P, c * P + P)
                    last = product(XB[:, c * P:c * P + P], oT[:, q % 2, 0, tok], oT[:, q % 2, 1, tok],
                                   wh(WO, q * P, P), wl(WO, q * P, P), q == 0 and c == 0, q == PAIRS - 1, True)
                last.then_inc(y_mm, 1)

            def attend(n, more):
                pe.wait_ge(max_placed, 32 * (n + 1))
                wait(pe, sg_done, n * EP)
                wait(pe, up_done, n * EP)
                pe.wait_ge(rowmaxT_ready, n + 1)
                for step in range(H + TURN + 1):
                    if step < H:
                        scores(n, step)
                    if 0 <= step - LAG < H:
                        times_v(n, step - LAG)
                    h = step - TURN
                    if 0 <= h < H and h % 2 == 1:
                        turn_heads(n, h // 2)
                    if 0 <= h - 1 < H and h % 2 == 0:
                        times_wo(n, (h - 1) // 2)
                    if more and step == H:
                        project(n + 1)
                    tail = step - H - 1
                    if more and 0 <= tail < len(TAIL_AT):
                        project_units(n + 1, tail_from(tail), TAIL_AT[tail])

            def route(n, more):
                def projections(first, end):
                    if more:
                        project_units(n + 1, first, end)
                projections(TAIL_AT[-1], TURN_AT)
                pe.wait_ge(oT_ready, (n + 1) * PAIRS)
                pe.wait_ge(h2_lo, n + 1)
                transpose_split(expert_bank, split_hl).then_inc(h2T_mm, 1)
                projections(TURN_AT, LOGITS_AT)
                pe.wait_ge(h2T_ready, n + 1)
                for c in range(C):
                    tok = slice(c * P, c * P + P)
                    last = product(logit_bank[:, c * NE:(c + 1) * NE], h2T[:, 0, tok], h2T[:, 1, tok], wh(WG, 0, NE), wl(WG, 0, NE))
                last.then_inc(logit_mm, 1)
                projections(LOGITS_AT, SPREAD_AT)
                pe.wait_ge(comb_split, 5 * n + 5)
                for c in range(C):
                    last = pe.transpose(half(comb_bank)[:, c * P:c * P + P], comb_parts[:, c].rearrange("p a e -> p (a e)"), ident[:, :])
                last.then_inc(combT_mm, 1)
                projections(SPREAD_AT, NPROJ)

            def gate(n, j):
                if j >= 2:
                    pe.wait_ge(sg_done, n * EP + j - 1)
                product(gate_banks[j % 2][:, :], wh(WGU, j * 2 * P, P), wl(WGU, j * 2 * P, P), h2T[:, 0, :], h2T[:, 1, :]).then_inc(g_mm, 1)

            def up_product(n, j):
                if j >= 2:
                    pe.wait_ge(up_done, n * EP + j - 1)
                product(up_banks[j % 2][:, :], wh(WGU, j * 2 * P + P, P), wl(WGU, j * 2 * P + P, P),
                        h2T[:, 0, :], h2T[:, 1, :]).then_inc(u_mm, 1)

            def spread_weights(n, j):
                if j >= 1:
                    pe.wait_ge(a32_done, n * EP + j)
                mm(weight_bank[:, :], select[:, j, :], combT[:, :], True, True).then_inc(wgt_mm, 1)

            def experts_down(n, j):
                pe.wait_ge(a_lo_done, n * EP + j + 1)
                if j == 0:
                    pe.wait_ge(y0_done, n + 1)
                for c in range(C):
                    tok = slice(c * P, c * P + P)
                    last = product(XB[:, c * P:c * P + P], a_hi[:, j % 3, tok], a_lo[:, j % 3, tok],
                                   wh(WD, j * D, D), wl(WD, j * D, D), j == 0 and c == 0, j == EP - 1, True)
                last.then_inc(down_mm, 1)

            def experts(n, projected):
                if projected:
                    pe.wait_ge(proj_lo, (n + 2) * NPROJ - 1)
                for j in range(EP + DOWN_LAG):
                    maxima = maxima_of(j) if projected else []
                    if projected and j == 1:
                        pe.wait_ge(proj_lo, (n + 2) * NPROJ)
                    if j < EP:
                        gate(n, j)
                    if j == 0:
                        pe.wait_ge(combT_ready, n + 1)
                        pe.wait_ge(logits_done, n + 1)
                    if 1 <= j <= EP:
                        spread_weights(n, j - 1)
                    for h, u in maxima[0:1]:
                        max_scores(n + 1, h, u)
                    if j < EP:
                        up_product(n, j)
                    for h, u in maxima[1:2]:
                        max_scores(n + 1, h, u)
                    if j >= DOWN_LAG:
                        experts_down(n, j - DOWN_LAG)
                    for h, u in maxima[2:]:
                        max_scores(n + 1, h, u)
                    if projected and j == MAX_END:
                        turn_maxima(n + 1)

            pe.wait_ge(consts_loaded, 80)
            pe.wait_ge(w_lo_done, 7)
            project(0)
            project_units(0, 0, NPROJ)
            for h in range(H):
                for u in range(MAX_UNITS):
                    max_scores(0, h, u)
            turn_maxima(0)

            def sequence(n, more):
                attend(n, more)
                route(n, more)
                experts(n, more)

            sequence(0, True)
            with pe.Fori(1, B - 1) as i:
                sequence(i, True)
            sequence(B - 1, False)

        @block.scalar
        def _(act):
            def project(n):
                act.wait_ge(hT_mm, n + 1)
                wait(act, proj_mm, n * NPROJ)
                act.activation(hT[:, :, :].rearrange("p a s -> p (a s)"), half(input_bank), ACT.Copy).then_inc(hT_ready, 1)

            def project_high(n, first, end):
                for k in range(first, end):
                    bank = proj_banks[k % 4]
                    act.wait_ge(proj_mm, n * NPROJ + k + 1)
                    if k == NKQ:
                        wait(act, pv_mm, n * H)
                    if k >= NKQ:
                        c, side = (k - NKQ) // 2, k % 2
                        act.activation(v_hi[:, c, 8 * side:8 * side + 8, 0:E], bank[:, :].rearrange("p (h e) -> p h e", h=8),
                                       ACT.Copy).then_inc(proj_hi, 1)
                    else:
                        pair, w = k // 2, k % 2
                        g = pair // 2
                        if pair % 2 == 0 and w == 0:
                            wait(act, placed[g - 2] if g >= 2 else placed[g + 2], 192 * (n + 1) if g >= 2 else 192 * n)
                        act.activation(nat_hi[:, g % 2, w, pair % 2, :], bank[:, :], ACT.Copy).then_inc(proj_hi, 1)

            def copy_maxima(n):
                act.wait_ge(rowmaxT_mm, n + 1)
                wait(act, max_placed, 32 * n)
                act.activation(rowmaxT[:, :], half(G0)[0:2 * H, 0:S], ACT.Copy).then_inc(rowmaxT_ready, 1)

            def attend(n, more):
                for step in range(H + TURN + 1):
                    if step < H:
                        for u, (at, cols) in enumerate(((0, 512), (512, 512), (1024, 256))):
                            act.wait_ge(score_mm, n * H * UNITS + step * UNITS + u + 1)
                            if u == 0:
                                used = max(0, step - 2)
                                wait(act, p_lo_dve, n * H + used)
                                wait(act, p_lo_pool, n * H + used)
                            act.activation(p32[:, step % 3, at:at + cols], score_banks[u][:, 0:cols], ACT.Exp,
                                           scale=back[:, SC_SCORE:SC_SCORE + 1]).then_inc(exp_done, 1)
                    h = step - LAG - 1
                    if 0 <= h < H:
                        q, ab = h // 2, h % 2
                        if ab == 0:
                            wait(act, oT_mm, n * PAIRS + max(0, q - 1))
                        act.wait_ge(o32_done, n * H + h + 1)
                        act.activation(o_hl[:, q % 2, 0, :, E * ab:E * ab + E], o32[:, h % 2], ACT.Copy).then_inc(o_hi_done, 1)
                    h = step - TURN
                    if 0 <= h < H and h % 2 == 1:
                        copy_oT(n, h // 2)
                    if more and step == H:
                        project(n + 1)
                    tail = step - H - 1
                    if more and 0 <= tail < len(TAIL_AT):
                        project_high(n + 1, tail_from(tail), TAIL_AT[tail])

            def copy_oT(n, q):
                act.wait_ge(oT_mm, n * PAIRS + q + 1)
                wait(act, y_mm, n * PAIRS + max(0, q - 1))
                act.activation(oT[:, q % 2].rearrange("p a s -> p (a s)"), half(oT_banks[q % 2]), ACT.Copy).then_inc(oT_ready, 1)

            def route(n, more):
                def projections(first, end):
                    if more:
                        project_high(n + 1, first, end)
                projections(TAIL_AT[-1], TURN_AT)
                act.wait_ge(h2T_mm, n + 1)
                wait(act, u_mm, n * EP)
                act.activation(h2T[:, :, :].rearrange("p a s -> p (a s)"), half(expert_bank), ACT.Copy).then_inc(h2T_ready, 1)
                projections(TURN_AT, EXP_AT)
                act.wait_ge(shift_done, n + 1)
                wait(act, exm_done, n)
                act.activation(ex[:, :, :], shifted[:, :, :], ACT.Exp).then_inc(ex_done, 1)
                projections(EXP_AT, SPREAD_AT)
                act.wait_ge(combT_mm, n + 1)
                wait(act, wgt_mm, n * EP)
                act.activation(combT[:, :], half(comb_bank)[:, 0:S], ACT.Copy).then_inc(combT_ready, 1)
                projections(SPREAD_AT, NPROJ)

            def experts(n, more):
                for j in range(EP + 2):
                    if j < EP:
                        act.wait_ge(g_mm, n * EP + j + 1)
                        wait(act, su_done, n * EP + max(0, j - 1))
                        act.activation(sg[:, j % 2, :], gate_banks[j % 2][:, :], ACT.Silu, scale=w_back[:, WGU:WGU + 1]).then_inc(sg_done, 1)
                        act.wait_ge(u_mm, n * EP + j + 1)
                        wait(act, a32_done, n * EP + max(0, j - 2))
                        act.activation(up[:, j % 3, :], up_banks[j % 2][:, :], ACT.Copy).then_inc(up_done, 1)
                    k = j - 2
                    if k >= 0:
                        act.wait_ge(a32_done, n * EP + k + 1)
                        wait(act, down_mm, n * EP + max(0, k - 2))
                        act.activation(a_hi[:, k % 3, :], a32[:, k % 3, :], ACT.Copy).then_inc(a_hi_done, 1)
                    if more and j == MAX_END + 1:
                        copy_maxima(n + 1)

            act.wait_ge(w_scaling, 7)
            for w in range(7):
                act.activation(wh(w, 0, WCOLS[w]), raw[:, WAT[w]:WAT[w] + WCOLS[w]], ACT.Copy, scale=w_scale[:, w:w + 1]).then_inc(w_hi_done, 1)
            project(0)
            project_high(0, 0, NPROJ)
            copy_maxima(0)

            def sequence(n, more):
                attend(n, more)
                route(n, more)
                experts(n, more)

            sequence(0, True)
            with act.Fori(1, B - 1) as i:
                sequence(i, True)
            sequence(B - 1, False)

        @block.vector
        def _(dve):
            def norm_stats(n, which, src):
                wait(dve, ln_mv[which], C * n)
                for c in range(C):
                    dve.bn_stats(stats[:, which, c, :], src[:, c, :]).then_inc(ln_stats[which], 1)
                dve.wait_ge(ln_stats[which], C * (n + 1))
                wait(dve, ln_out[which], C * n)
                wait(dve, ln_var[which], n)
                apart(dve)
                for c in range(C):
                    dve.bn_aggr(mv[:, which, c, :], stats[:, which, c, :]).then_inc(ln_mv[which], 1)

            def norm_apply(n, which, src, dst):
                dve.wait_ge(ln_rstd[which], n + 1)
                for c in range(C):
                    dve.tensor_scalar(dst[:, c, :], src[:, c, :], mv[:, which, c, 0:1], rstd[:, which, c:c + 1],
                                      ALU.subtract, ALU.mult).then_inc(ln_out[which], 1)

            def split_norm(n, which, src, hl, hi_sem, lo_sem):
                dve.wait_ge(ln_out[which], C * (n + 1))
                dve.tensor_copy(hl[:, 0], src).then_inc(hi_sem, 1)
                dve.wait_ge(hi_sem, n + 1)
                dve.tensor_tensor(hl[:, 1], src, hl[:, 0], ALU.subtract).then_inc(lo_sem, 1)

            def normalise_input(n):
                dve.wait_ge(x_loaded, 16 * (n + 1))
                norm_stats(n, 0, xt)
                wait(dve, cur_copied, 2 * n)
                norm_apply(n, 0, xt, h32)
                wait(dve, h2T_mm, n - 1)
                split_norm(n, 0, h32[:, :, :], split_hl, h_hi, h_lo)

            def project_low(n, first, end):
                for k in range(first, end):
                    bank = proj_banks[k % 4]
                    dve.wait_ge(proj_hi, n * NPROJ + k + 1)
                    if k == NKQ:
                        wait(dve, pv_mm, n * H)
                    if k >= NKQ:
                        c, side = (k - NKQ) // 2, k % 2
                        dve.tensor_tensor(v_lo[:, c, 8 * side:8 * side + 8, :], bank[:, :].rearrange("p (h e) -> p h e", h=8),
                                          v_hi[:, c, 8 * side:8 * side + 8, 0:E], ALU.subtract).then_inc(proj_lo, 1)
                    else:
                        pair, w = k // 2, k % 2
                        g = pair // 2
                        if pair % 2 == 0 and w == 0:
                            wait(dve, placed[g - 2] if g >= 2 else placed[g + 2], 192 * (n + 1) if g >= 2 else 192 * n)
                        dve.tensor_tensor(nat_lo[:, g % 2, w, pair % 2, :], bank[:, :], nat_hi[:, g % 2, w, pair % 2, :],
                                          ALU.subtract).then_inc(proj_lo, 1)

            def row_maximum(n, h, u):
                k, hs = h * MAX_UNITS + u, (h % 2) * PAIRS + h // 2
                dve.wait_ge(max_mm, n * H * MAX_UNITS + k + 1)
                wait(dve, max_done, n * H * MAX_UNITS + max(0, k - 1))
                if k == 0:
                    wait(dve, rowmax_lo, n)
                apart(dve)
                for c in MAX_CHUNKS[u]:
                    cols, at = (c + 1) * P, max_col(c)
                    last = dve.tensor_tensor_reduce(max_junk[:, k % 2, at:at + cols], max_banks[k % 2][:, at:at + cols], mask[:, S - cols:S],
                                                    1.0, NEG, ALU.add, ALU.max, rowmax[:, c, hs:hs + 1])
                last.then_inc(max_done, 1)

            def split_maxima(n):
                dve.wait_ge(max_done, (n + 1) * H * MAX_UNITS)
                wait(dve, rowmaxT_mm, n)
                dve.tensor_scalar(rowmax_hl[:, :, 0, :], rowmax[:, :, :], -1.0 / MAX_UNIT, None, ALU.mult).then_inc(rowmax_hi, 1)
                dve.wait_ge(rowmax_hi, n + 1)
                dve.scalar_tensor_tensor(rowmax_hl[:, :, 1, :], rowmax[:, :, :], -1.0 / MAX_UNIT, rowmax_hl[:, :, 0, :],
                                         ALU.mult, ALU.subtract).then_inc(rowmax_lo, 1)

            def attend(n, more):
                for step in range(H + LAG + 2):
                    if more and step == NORMALISE_AT:
                        normalise_input(n + 1)
                    h = step - LAG - 2
                    if 0 <= h < H:
                        low(n, h)
                    h = step - LAG - 1
                    if 0 <= h < H:
                        bank = pv_banks[h % 2][:, 0:C * (E + 1)].rearrange("p (c e) -> p c e", c=C)
                        dve.wait_ge(pv_mm, n * H + h + 1)
                        dve.reciprocal(rden[:, h % 2, :].rearrange("p (c a) -> p c a", a=1), bank[:, :, E:E + 1]).then_inc(rden_done, 1)
                        dve.wait_ge(rden_done, n * H + h + 1)
                        wait(dve, o_hi_done, n * H + max(0, h - 1))
                        wait(dve, o_lo_done, n * H + max(0, h - 1))
                        dve.tensor_tensor(o32[:, h % 2], bank[:, :, 0:E],
                                          rden[:, h % 2, :].rearrange("p (c a) -> p c a", a=1).to_broadcast([P, C, E]), ALU.mult).then_inc(o32_done, 1)
                    h = step - 1
                    if 0 <= h < H:
                        dve.wait_ge(masked, n * H + h + 1)
                        wait(dve, pv_mm, n * H + max(0, h - 2))
                        dve.tensor_copy(p_hi[:, h % 3, :], p32[:, h % 3, :]).then_inc(p_hi_done, 1)
                        dve.wait_ge(p_hi_done, n * H + h + 1)
                        dve.tensor_tensor(p_lo[:, h % 3, 0:S], p32[:, h % 3, 0:S], p_hi[:, h % 3, 0:S], ALU.subtract).then_inc(p_lo_dve, 1)
                    tail = step - H - 1
                    if more and 0 <= tail < len(TAIL_AT):
                        project_low(n + 1, tail_from(tail), TAIL_AT[tail])

            def low(n, h):
                q, ab = h // 2, h % 2
                cols = slice(E * ab, E * ab + E)
                dve.wait_ge(o_hi_done, n * H + h + 1)
                wait(dve, oT_mm, n * PAIRS + max(0, q - 1))
                dve.tensor_tensor(o_hl[:, q % 2, 1, :, cols], o32[:, h % 2], o_hl[:, q % 2, 0, :, cols], ALU.subtract).then_inc(o_lo_done, 1)

            def residual(n, more):
                dve.wait_ge(y_mm, PAIRS * (n + 1))
                dve.wait_ge(cur_copied, 2 * n + 2)
                wait(dve, out_stored, 16 * n)
                dve.scalar_tensor_tensor(y0[:, :, :], XB[:, :].rearrange("p (c d) -> p c d", c=C), back[:, SC_Y:SC_Y + 1],
                                         h_cur[:, :, :], ALU.mult, ALU.add).then_inc(y0_done, 1)
                dve.wait_ge(y0_done, n + 1)
                norm_stats(n, 1, y0)
                if more:
                    project_low(n + 1, TAIL_AT[-1], NORM_AT[0])
                wait(dve, yg_done, n)
                norm_apply(n, 1, y0, y0)
                dve.wait_ge(ln_out[1], C * (n + 1))
                wait(dve, x1_done, n)
                dve.tensor_tensor(y0[:, :, :], y0[:, :, :], gam[:, :, :].to_broadcast([P, C, D]), ALU.mult).then_inc(yg_done, 1)
                dve.wait_ge(yg_done, n + 1)
                wait(dve, out_ready, n)
                dve.tensor_tensor(x1[:, :, :], y0[:, :, :], xb_cur[:, :, :], ALU.add).then_inc(x1_done, 1)
                dve.wait_ge(x1_done, n + 1)
                norm_stats(n, 2, x1)
                if more:
                    project_low(n + 1, NORM_AT[0], NORM_AT[1])
                wait(dve, h2_lo, n)
                dve.wait_ge(x1_done, n + 1)
                norm_apply(n, 2, x1, y0)
                dve.wait_ge(hT_mm, n + 2 if more else n + 1)
                split_norm(n, 2, y0[:, :, :], split_hl, h2_hi, h2_lo)

            def route(n, more):
                if more:
                    project_low(n + 1, NORM_AT[1], CHOOSE_AT)
                dve.wait_ge(logit_mm, n + 1)
                wait(dve, shift_done, n)
                wait(dve, chosen_done, n)
                dve.tensor_scalar(logits[:, :, :], logit_bank[:, 0:C * NE].rearrange("p (c e) -> p c e", c=C), w_back[:, WG:WG + 1], None,
                                  ALU.mult).then_inc(logits_done, 1)
                dve.wait_ge(logits_done, n + 1)
                wait(dve, drop_done, C * n)
                apart(dve)
                for c in range(C):
                    dve.max(top8[:, c, :], logits[:, c, :]).then_inc(top_done, 1)
                dve.wait_ge(top_done, C * (n + 1))
                apart(dve)
                for c in range(C):
                    dve.match_replace(dropped[:, c, :], top8[:, c, :], logits[:, c, :], NEG).then_inc(drop_done, 1)
                wait(dve, ex_done, n)
                dve.tensor_tensor(shifted[:, :, :], logits[:, :, :], top8[:, :, 0:1].to_broadcast([P, C, NE]), ALU.subtract).then_inc(shift_done, 1)
                dve.wait_ge(drop_done, C * (n + 1))
                wait(dve, exm_done, n)
                dve.tensor_tensor(chosen[:, :, :], dropped[:, :, :], logits[:, :, :], ALU.not_equal).then_inc(chosen_done, 1)
                if more:
                    project_low(n + 1, CHOOSE_AT, WEIGH_AT)
                dve.wait_ge(chosen_done, n + 1)
                dve.wait_ge(ex_done, n + 1)
                wait(dve, comb_done, n)
                dve.tensor_tensor(exm[:, :, :], ex[:, :, :], chosen[:, :, :], ALU.mult).then_inc(exm_done, 1)
                dve.wait_ge(exm_done, n + 1)
                wait(dve, exinv_done, n)
                dve.tensor_reduce(exsum[:, :], exm[:, :, :], AX.X, ALU.add).then_inc(exsum_done, 1)
                dve.wait_ge(exsum_done, n + 1)
                dve.reciprocal(exinv[:, :], exsum[:, :]).then_inc(exinv_done, 1)
                dve.wait_ge(exinv_done, n + 1)
                wait(dve, comb_split, 5 * n)
                wait(dve, combT_mm, n)
                dve.tensor_tensor(comb[:, :, :], exm[:, :, :], exinv[:, :].rearrange("p (c a) -> p c a", a=1).to_broadcast([P, C, NE]),
                                  ALU.mult).then_inc(comb_done, 1)
                dve.wait_ge(comb_done, n + 1)
                dve.tensor_copy(comb_parts[:, :, 0, :], comb[:, :, :]).then_inc(comb_split, 1)
                dve.wait_ge(comb_split, 5 * n + 1)
                dve.tensor_tensor(comb_rest[:, :, :], comb[:, :, :], comb_parts[:, :, 0, :], ALU.subtract).then_inc(comb_split, 1)
                dve.wait_ge(comb_split, 5 * n + 2)
                dve.tensor_copy(comb_parts[:, :, 1, :], comb_rest[:, :, :]).then_inc(comb_split, 1)
                dve.wait_ge(comb_split, 5 * n + 3)
                dve.tensor_tensor(comb_parts[:, :, 2, :], comb_rest[:, :, :], comb_parts[:, :, 1, :], ALU.subtract).then_inc(comb_split, 2)
                if more:
                    project_low(n + 1, WEIGH_AT, NPROJ)

            def experts(n, more):
                for j in range(EP + 1):
                    maxima = maxima_of(j) if more else []
                    if more and j == MAX_END:
                        split_maxima(n + 1)
                    for h, u in maxima[0:2]:
                        row_maximum(n + 1, h, u)
                    k = j - 1
                    if k >= 0:
                        dve.wait_ge(su_done, n * EP + k + 1)
                        dve.wait_ge(wgt_mm, n * EP + k + 1)
                        wait(dve, a_hi_done, n * EP + max(0, k - 2))
                        wait(dve, a_lo_done, n * EP + max(0, k - 2))
                        dve.tensor_tensor(a32[:, k % 3, :], weight_bank[:, :], up[:, k % 3, :], ALU.mult).then_inc(a32_done, 1)
                    for h, u in maxima[2:]:
                        row_maximum(n + 1, h, u)
                dve.wait_ge(down_mm, EP * (n + 1))
                dve.wait_ge(h2_lo, n + 1)
                dve.scalar_tensor_tensor(y0[:, :, :], XB[:, :].rearrange("p (c d) -> p c d", c=C), back[:, SC_OUT:SC_OUT + 1],
                                         x1[:, :, :], ALU.mult, ALU.add).then_inc(out_ready, 1)

            normalise_input(0)
            dve.memset(w_absmax[:, :], 1.0).then_inc(absmax_set, 1)
            dve.wait_ge(absmax_set, 1)
            for w in range(7):
                dve.wait_ge(w_loaded[w], 16)
                dve.tensor_reduce(w_absmax[:, w:w + 1], raw[:, WAT[w]:WAT[w] + WCOLS[w]], AX.X, ALU.max,
                                  apply_absolute_value=True).then_inc(w_maxed, 1)
            dve.wait_ge(w_allmaxed, 1)
            dve.tensor_scalar(w_allmax[:, :], w_allmax[:, :], 2.0 ** -100, None, ALU.max).then_inc(w_scaling, 1)
            dve.wait_ge(w_scaling, 1)
            dve.tensor_scalar(w_pow[:, :].bitcast(I32), w_allmax[:, :].bitcast(I32), 0x7F800000, None, ALU.bitwise_and).then_inc(w_scaling, 1)
            dve.wait_ge(w_scaling, 2)
            dve.tensor_scalar(w_back[:, :], w_pow[:, :], 0.125, None, ALU.mult).then_inc(w_scaling, 1)
            dve.wait_ge(w_scaling, 3)
            dve.reciprocal(w_scale[:, :], w_back[:, :]).then_inc(w_scaling, 1)

            def pair_product(dst, a, b, factor):
                return dve.scalar_tensor_tensor(back[:, dst:dst + 1], a, factor, b, ALU.mult, ALU.mult)

            def wb(w):
                return w_back[:, w:w + 1]
            pair_product(SC_SCORE, wb(WQ), wb(WK), float(E) ** -0.5).then_inc(w_scaling, 1)
            pair_product(SC_Y, wb(WV), wb(WO), 1.0).then_inc(w_scaling, 1)
            pair_product(SC_OUT, wb(WGU), wb(WD), 1.0 / COMB_SHIFT).then_inc(w_scaling, 1)
            dve.wait_ge(w_scaling, 7)
            for w in range(7):
                src = raw[:, WAT[w]:WAT[w] + WCOLS[w]]
                scale = w_scale[:, w:w + 1]
                dve.wait_ge(w_hi_done, w + 1)
                dve.scalar_tensor_tensor(wl(w, 0, WCOLS[w]), src, scale, wh(w, 0, WCOLS[w]), ALU.mult, ALU.subtract).then_inc(w_lo_done, 1)
            dve.wait_ge(w_lo_done, 7)
            dve.wait_ge(consts_set, 4)
            dve.wait_ge(consts_loaded, 80)

            project_low(0, 0, NPROJ)
            for h in range(H):
                for u in range(MAX_UNITS):
                    row_maximum(0, h, u)
            split_maxima(0)

            def sequence(n, more):
                attend(n, more)
                residual(n, more)
                route(n, more)
                experts(n, more)

            sequence(0, True)
            with dve.Fori(1, B - 1) as i:
                sequence(i, True)
            sequence(B - 1, False)

        @block.gpsimd
        def _(pool):
            def inverse_deviation(n, which, eps):
                pool.wait_ge(ln_mv[which], C * (n + 1))
                apart(pool)
                pool.tensor_scalar(var_eps[:, which, :].rearrange("p (c a) -> p c a", a=1), mv[:, which, :, 1:2], eps, 0.0, ALU.add, ALU.add).then_inc(ln_var[which], 1)
                pool.wait_ge(ln_var[which], n + 1)
                wait(pool, ln_out[which], C * n)
                pool.tensor_tensor(rstd[:, which, :], var_eps[:, which, :], minus_half[:, :], ALU.pow).then_inc(ln_rstd[which], 1)

            def normalise_input(n):
                inverse_deviation(n, 0, LN_EPS)

            def keep_current(n):
                pool.wait_ge(h_lo, n + 1)
                wait(pool, x1_done, n)
                apart(pool)
                pool.tensor_copy(h_cur[:, :, :], h32[:, :, :]).then_inc(cur_copied, 1)
                pool.wait_ge(x_loaded, 16 * (n + 1))
                pool.tensor_tensor(xb_cur[:, :, :], xt[:, :, :], bet[:, :, :].to_broadcast([P, C, D]), ALU.add).then_inc(cur_copied, 1)

            def attend(n, more):
                for step in range(H + 1):
                    if more and step == NORMALISE_AT:
                        normalise_input(n + 1)
                    if step < H:
                        pool.wait_ge(exp_done, n * H * UNITS + UNITS * (step + 1))
                        apart(pool)
                        p = p32[:, step % 3, :]
                        keep = dict(compare_op=ALU.is_ge, fill=0.0, base=0, channel_multiplier=-1)
                        far = p[:, 0:1024].rearrange("p (a s) -> p a s", a=2)[:, :, 0:P]
                        pool.affine_select(far, far, pattern=[[0, 2], [1, P]], **keep).then_inc(diag_pair, 1)
                        near = p[:, 896:1152].rearrange("p (a s) -> p a s", a=2)
                        pool.affine_select(near, near, pattern=[[0, 2], [1, P]], **keep).then_inc(masked, 1)
                    h = step - 1
                    if h >= 0:
                        pool.wait_ge(p_hi_done, n * H + h + 1)
                        wait(pool, pv_mm, n * H + max(0, h - 2))
                        pool.tensor_tensor(p_lo[:, h % 3, S:PCOLS], p32[:, h % 3, S:PCOLS], p_hi[:, h % 3, S:PCOLS], ALU.subtract).then_inc(p_lo_pool, 1)

            def experts(n):
                for j in range(EP + 2):
                    if j < EP:
                        pool.wait_ge(up_done, n * EP + j + 1)
                        pool.wait_ge(sg_done, n * EP + j + 1)
                        pool.tensor_tensor(up[:, j % 3, :], sg[:, j % 2, :], up[:, j % 3, :], ALU.mult).then_inc(su_done, 1)
                    k = j - 2
                    if k >= 0:
                        pool.wait_ge(a_hi_done, n * EP + k + 1)
                        wait(pool, down_mm, n * EP + max(0, k - 2))
                        pool.tensor_tensor(a_lo[:, k % 3, :], a32[:, k % 3, :], a_hi[:, k % 3, :], ALU.subtract).then_inc(a_lo_done, 1)

            pool.memset(minus_half[:, :], -0.5).then_inc(pool_set, 1)
            pool.memset(v_hi[:, :, :, E:E + 1], 1.0).then_inc(consts_set, 1)
            pool.memset(comb_parts[:, :, 3, :], 0.0).then_inc(consts_set, 1)
            pool.wait_ge(pool_set, 1)
            pool.wait_ge(consts_set, 2)
            pool.memset(QB[E:P].rearrange("p a b s -> p (a b s)").bitcast(F32), 0.0).then_inc(consts_set, 1)
            pool.wait_ge(consts_set, 3)
            normalise_input(0)
            pool.wait_ge(w_maxed, 7)
            pool.partition_all_reduce(w_allmax[:, :], w_absmax[:, :], P, bass.bass_isa.ReduceOp.absmax).then_inc(w_allmaxed, 1)
            pool.wait_ge(w_allmaxed, 1)
            pool.wait_ge(w_lo_done, 5)
            pool.memset(KB[E:P].rearrange("p a b s -> p (a b s)").bitcast(F32), 0.0).then_inc(zeros_set, 1)
            pool.wait_ge(zeros_set, 1)
            pool.memset(KB[E:E + 2].rearrange("p a b s -> p (a b s)"), MAX_UNIT).then_inc(consts_set, 1)
            pool.wait_ge(consts_set, 4)
            pool.wait_ge(consts_loaded, 80)
            keep_current(0)

            def sequence(n, more):
                attend(n, more)
                inverse_deviation(n, 1, ATTN_LN_EPS)
                inverse_deviation(n, 2, LN_EPS)
                if more:
                    keep_current(n + 1)
                experts(n)

            sequence(0, True)
            with pool.Fori(1, B - 1) as i:
                sequence(i, True)
            sequence(B - 1, False)


_INS = ("L0_attn_x", "L0_attn_Wq", "L0_attn_Wk", "L0_attn_Wv", "L0_attn_Wo", "L0_attn_gamma", "L0_attn_beta",
        "L0_ffn_gate_w", "L0_ffn_gate_up_w", "L0_ffn_down_w")


def kernel(**inputs):
    import concourse.bacc as bacc
    from concourse.bass_utils import run_bass_kernel_spmd

    x, wq, wk, wv, wo, gamma, beta, gate_w, gate_up_w, down_w = (np.asarray(inputs[n]) for n in _INS)
    cont = np.ascontiguousarray

    def by_width(w):
        return cont(w.transpose(1, 0, 2).reshape(D, H * E))
    gu = gate_up_w.reshape(EP, 2, 2, ED, D).transpose(4, 0, 2, 1, 3)
    select = np.zeros((P, EP, P), np.float16)
    for part in range(3):
        for e in range(NE):
            select[part * NE + e, e // 2, (e % 2) * ED:(e % 2) * ED + ED] = COMB_SHIFT
    col = np.arange(S) - (S - P)
    arrays = {
        "x": cont(x), "wq": by_width(wq), "wk": by_width(wk), "wv": by_width(wv),
        "wo": cont(wo.reshape(PAIRS, P, D).transpose(1, 0, 2).reshape(P, PAIRS * D)),
        "gamma": cont(np.broadcast_to(gamma, (P, 1, D))), "beta": cont(np.broadcast_to(beta, (P, 1, D))),
        "gate": cont(gate_w.T), "gate_up": cont(gu.reshape(D, EP * 4 * ED)),
        "down": cont(down_w.reshape(EP, 2, D, ED).transpose(1, 3, 0, 2).reshape(P, EP * D)),
        "ident": np.eye(P, dtype=np.float16),
        "mask": np.where(col[None, :] > np.arange(P)[:, None], np.float32(NEG), np.float32(0.0)),
        "select": select,
    }
    nc = bacc.Bacc("TRN2", target_bir_lowering=False, num_devices=1)
    args = [nc.dram_tensor(f"in_{n}", a.shape, mybir.dt.from_np(a.dtype), kind="ExternalInput").ap() for n, a in arrays.items()]
    out = nc.dram_tensor("out_y", (B, S, D), F32, kind="ExternalOutput").ap()
    layer(nc, *args, out)
    r = run_bass_kernel_spmd(nc, [{f"in_{n}": a for n, a in arrays.items()}], core_ids=[0])
    return r.results[0]["out_y"]
```
